# Optimizing a Trainium2 kernel written in Bass

```python
import numpy as np
import jax
import jax.numpy as jnp

def _softmax(x, axis=-1):
    return jax.nn.softmax(x, axis=axis)

def _gelu(x):
    return jax.nn.gelu(x, approximate=True)

def _silu(x):
    return jax.nn.silu(x)

def _sigmoid(x):
    return jax.nn.sigmoid(x)

def _layernorm(x, axis=-1, eps=1e-05):
    m = jnp.mean(x, axis=axis, keepdims=True)
    v = jnp.var(x, axis=axis, keepdims=True)
    return (x - m) / jnp.sqrt(v + eps)

def _scatter_add(tgt, idx, src, axis=0):
    return tgt.at[idx].add(src)

def _segment_sum(src, seg, n):
    return jax.ops.segment_sum(src, seg, n)
kernel_name = 'mk_dlrm_tower_d1_rec_r8_9c14e2'

def setup_inputs(seed: int=0):
    np.random.seed(seed)
    _w = jnp.asarray

    def _rec_inputs():
        import jax
        import jax.numpy as jnp
        _tk = jax.random.key(seed)
        ids = jnp.stack([jax.random.randint(jax.random.fold_in(_tk, 200 + f), (2048,), 0, v, jnp.int32) for f, v in enumerate([1250, 1000, 12500, 1250, 125000, 125000, 125000, 1000, 12500, 1000, 1250, 1250, 12500, 12500, 1250, 12500, 12500, 1250, 1250, 1250, 1250, 1250, 1250, 1250, 1000, 12500])], axis=1)
        tbl_0 = 0.05 * jax.random.normal(jax.random.fold_in(_tk, 500 + 0), (1250, 64), jnp.float32)
        tbl_1 = 0.05 * jax.random.normal(jax.random.fold_in(_tk, 500 + 1), (1000, 64), jnp.float32)
        tbl_2 = 0.05 * jax.random.normal(jax.random.fold_in(_tk, 500 + 2), (12500, 64), jnp.float32)
        tbl_3 = 0.05 * jax.random.normal(jax.random.fold_in(_tk, 500 + 3), (1250, 64), jnp.float32)
        tbl_4 = 0.05 * jax.random.normal(jax.random.fold_in(_tk, 500 + 4), (125000, 64), jnp.float32)
        tbl_5 = 0.05 * jax.random.normal(jax.random.fold_in(_tk, 500 + 5), (125000, 64), jnp.float32)
        tbl_6 = 0.05 * jax.random.normal(jax.random.fold_in(_tk, 500 + 6), (125000, 64), jnp.float32)
        tbl_7 = 0.05 * jax.random.normal(jax.random.fold_in(_tk, 500 + 7), (1000, 64), jnp.float32)
        tbl_8 = 0.05 * jax.random.normal(jax.random.fold_in(_tk, 500 + 8), (12500, 64), jnp.float32)
        tbl_9 = 0.05 * jax.random.normal(jax.random.fold_in(_tk, 500 + 9), (1000, 64), jnp.float32)
        tbl_10 = 0.05 * jax.random.normal(jax.random.fold_in(_tk, 500 + 10), (1250, 64), jnp.float32)
        tbl_11 = 0.05 * jax.random.normal(jax.random.fold_in(_tk, 500 + 11), (1250, 64), jnp.float32)
        tbl_12 = 0.05 * jax.random.normal(jax.random.fold_in(_tk, 500 + 12), (12500, 64), jnp.float32)
        tbl_13 = 0.05 * jax.random.normal(jax.random.fold_in(_tk, 500 + 13), (12500, 64), jnp.float32)
        tbl_14 = 0.05 * jax.random.normal(jax.random.fold_in(_tk, 500 + 14), (1250, 64), jnp.float32)
        tbl_15 = 0.05 * jax.random.normal(jax.random.fold_in(_tk, 500 + 15), (12500, 64), jnp.float32)
        tbl_16 = 0.05 * jax.random.normal(jax.random.fold_in(_tk, 500 + 16), (12500, 64), jnp.float32)
        tbl_17 = 0.05 * jax.random.normal(jax.random.fold_in(_tk, 500 + 17), (1250, 64), jnp.float32)
        tbl_18 = 0.05 * jax.random.normal(jax.random.fold_in(_tk, 500 + 18), (1250, 64), jnp.float32)
        tbl_19 = 0.05 * jax.random.normal(jax.random.fold_in(_tk, 500 + 19), (1250, 64), jnp.float32)
        tbl_20 = 0.05 * jax.random.normal(jax.random.fold_in(_tk, 500 + 20), (1250, 64), jnp.float32)
        tbl_21 = 0.05 * jax.random.normal(jax.random.fold_in(_tk, 500 + 21), (1250, 64), jnp.float32)
        tbl_22 = 0.05 * jax.random.normal(jax.random.fold_in(_tk, 500 + 22), (1250, 64), jnp.float32)
        tbl_23 = 0.05 * jax.random.normal(jax.random.fold_in(_tk, 500 + 23), (1250, 64), jnp.float32)
        tbl_24 = 0.05 * jax.random.normal(jax.random.fold_in(_tk, 500 + 24), (1000, 64), jnp.float32)
        tbl_25 = 0.05 * jax.random.normal(jax.random.fold_in(_tk, 500 + 25), (12500, 64), jnp.float32)
        _rk = jax.random.fold_in(_tk, 7)
        r_dense_t = 7.22013e-05 + 1.00017 * jax.random.normal(jax.random.fold_in(_rk, 101), (2048, 256), jnp.float32)
        W_top1 = 0.0360844 * jax.random.normal(jax.random.fold_in(_tk, 801), (768, 512), jnp.float32)
        W_top2 = 0.0441942 * jax.random.normal(jax.random.fold_in(_tk, 802), (512, 256), jnp.float32)
        W_top3 = 0.0625 * jax.random.normal(jax.random.fold_in(_tk, 803), (256, 1), jnp.float32)
        b_top1 = jnp.zeros((512,), jnp.float32)
        b_top2 = jnp.zeros((256,), jnp.float32)
        return (r_dense_t, ids, tbl_0, tbl_1, tbl_2, tbl_3, tbl_4, tbl_5, tbl_6, tbl_7, tbl_8, tbl_9, tbl_10, tbl_11, tbl_12, tbl_13, tbl_14, tbl_15, tbl_16, tbl_17, tbl_18, tbl_19, tbl_20, tbl_21, tbl_22, tbl_23, tbl_24, tbl_25, W_top1, b_top1, W_top2, b_top2, W_top3)
    r_dense_t, ids, tbl_0, tbl_1, tbl_2, tbl_3, tbl_4, tbl_5, tbl_6, tbl_7, tbl_8, tbl_9, tbl_10, tbl_11, tbl_12, tbl_13, tbl_14, tbl_15, tbl_16, tbl_17, tbl_18, tbl_19, tbl_20, tbl_21, tbl_22, tbl_23, tbl_24, tbl_25, W_top1, b_top1, W_top2, b_top2, W_top3 = _rec_inputs()

    def _L0_rec_setup():
        import jax, jax.numpy as jnp
        import numpy as np
        EPS = 1e-05
        NI = 33
        TRIL_I, TRIL_J = np.tril_indices(NI, k=-1)

        def layer_norm(x, g, b):
            m = jnp.mean(x, axis=-1, keepdims=True)
            v = jnp.mean(jnp.square(x - m), axis=-1, keepdims=True)
            return (x - m) * jax.lax.rsqrt(v + EPS) * g + b
        key = jax.random.key(seed)
        ks = jax.random.split(key, 8)
        B, D_DENSE, N_SP, D_SP = (4096, 256, 26, 64)
        E, PROJ, MAXD, NFLAT = (128, 32, 512, 528)
        dense_t = jax.random.normal(ks[0], (B, D_DENSE), dtype=jnp.float32)
        sparse_t = jax.random.normal(ks[1], (B, N_SP, D_SP), dtype=jnp.float32)
        Wd = jax.random.normal(ks[2], (E, D_DENSE), dtype=jnp.float32) / np.sqrt(D_DENSE)
        Ws = jax.random.normal(ks[3], (E, D_SP), dtype=jnp.float32) / np.sqrt(D_SP)
        Wsi = jax.random.normal(ks[4], (PROJ, N_SP), dtype=jnp.float32) / np.sqrt(N_SP)
        Wl = jax.random.normal(ks[5], (MAXD, NFLAT), dtype=jnp.float32) / np.sqrt(NFLAT)
        gd = jnp.ones((E,), jnp.float32)
        bd = jnp.zeros((E,), jnp.float32)
        gs = jnp.ones((E,), jnp.float32)
        bs = jnp.zeros((E,), jnp.float32)
        gsi = jnp.ones((PROJ,), jnp.float32)
        bsi = jnp.zeros((PROJ,), jnp.float32)
        gl = jnp.ones((MAXD,), jnp.float32)
        bl = jnp.zeros((MAXD,), jnp.float32)
        return {'dense_t': dense_t, 'sparse_t': sparse_t, 'Wd': Wd, 'gd': gd, 'bd': bd, 'Ws': Ws, 'gs': gs, 'bs': bs, 'Wsi': Wsi, 'gsi': gsi, 'bsi': bsi, 'Wl': Wl, 'gl': gl, 'bl': bl, 'dims_in_use': 384}
    _L0_rec_all = _L0_rec_setup()
    _L0_rec_in = {k: v for k, v in _L0_rec_all.items() if k in ('Wd', 'gd', 'bd', 'Ws', 'gs', 'bs', 'Wsi', 'gsi', 'bsi', 'Wl', 'gl', 'bl')}
    del _L0_rec_all
    return {'r_dense_t': r_dense_t, 'ids': ids, 'tbl_0': tbl_0, 'tbl_1': tbl_1, 'tbl_2': tbl_2, 'tbl_3': tbl_3, 'tbl_4': tbl_4, 'tbl_5': tbl_5, 'tbl_6': tbl_6, 'tbl_7': tbl_7, 'tbl_8': tbl_8, 'tbl_9': tbl_9, 'tbl_10': tbl_10, 'tbl_11': tbl_11, 'tbl_12': tbl_12, 'tbl_13': tbl_13, 'tbl_14': tbl_14, 'tbl_15': tbl_15, 'tbl_16': tbl_16, 'tbl_17': tbl_17, 'tbl_18': tbl_18, 'tbl_19': tbl_19, 'tbl_20': tbl_20, 'tbl_21': tbl_21, 'tbl_22': tbl_22, 'tbl_23': tbl_23, 'tbl_24': tbl_24, 'tbl_25': tbl_25, 'W_top1': W_top1, 'b_top1': b_top1, 'W_top2': W_top2, 'b_top2': b_top2, 'W_top3': W_top3, 'L0_rec_Wd': _L0_rec_in['Wd'], 'L0_rec_gd': _L0_rec_in['gd'], 'L0_rec_bd': _L0_rec_in['bd'], 'L0_rec_Ws': _L0_rec_in['Ws'], 'L0_rec_gs': _L0_rec_in['gs'], 'L0_rec_bs': _L0_rec_in['bs'], 'L0_rec_Wsi': _L0_rec_in['Wsi'], 'L0_rec_gsi': _L0_rec_in['gsi'], 'L0_rec_bsi': _L0_rec_in['bsi'], 'L0_rec_Wl': _L0_rec_in['Wl'], 'L0_rec_gl': _L0_rec_in['gl'], 'L0_rec_bl': _L0_rec_in['bl']}

def reference(r_dense_t, ids, tbl_0, tbl_1, tbl_2, tbl_3, tbl_4, tbl_5, tbl_6, tbl_7, tbl_8, tbl_9, tbl_10, tbl_11, tbl_12, tbl_13, tbl_14, tbl_15, tbl_16, tbl_17, tbl_18, tbl_19, tbl_20, tbl_21, tbl_22, tbl_23, tbl_24, tbl_25, W_top1, b_top1, W_top2, b_top2, W_top3, L0_rec_Wd, L0_rec_gd, L0_rec_bd, L0_rec_Ws, L0_rec_gs, L0_rec_bs, L0_rec_Wsi, L0_rec_gsi, L0_rec_bsi, L0_rec_Wl, L0_rec_gl, L0_rec_bl):
    import jax
    import jax.numpy as jnp

    def _L0_rec_ref(dense_t, sparse_t, Wd, gd, bd, Ws, gs, bs, Wsi, gsi, bsi, Wl, gl, bl, dims_in_use):
        import jax, jax.numpy as jnp
        import numpy as np
        EPS = 1e-05
        NI = 33
        TRIL_I, TRIL_J = np.tril_indices(NI, k=-1)

        def layer_norm(x, g, b):
            m = jnp.mean(x, axis=-1, keepdims=True)
            v = jnp.mean(jnp.square(x - m), axis=-1, keepdims=True)
            return (x - m) * jax.lax.rsqrt(v + EPS) * g + b
        x = layer_norm(dense_t @ Wd.T, gd, bd)
        y = layer_norm(jnp.einsum('bnd,ed->bne', sparse_t, Ws), gs, bs)
        y = jnp.einsum('bne,pn->bep', y, Wsi)
        y = layer_norm(y, gsi, bsi)
        y = jnp.swapaxes(y, 1, 2)
        T = jnp.concatenate([x[:, None, :], y], axis=1)
        Z = jnp.einsum('bnd,bmd->bnm', T, T)
        Zflat = Z[:, TRIL_I, TRIL_J]
        out = layer_norm(Zflat @ Wl.T, gl, bl)
        maxd = out.shape[-1]
        mask = (jnp.arange(maxd) < dims_in_use).astype(out.dtype)
        return out * mask
    e = jnp.stack([tbl_0[ids[:, 0]], tbl_1[ids[:, 1]], tbl_2[ids[:, 2]], tbl_3[ids[:, 3]], tbl_4[ids[:, 4]], tbl_5[ids[:, 5]], tbl_6[ids[:, 6]], tbl_7[ids[:, 7]], tbl_8[ids[:, 8]], tbl_9[ids[:, 9]], tbl_10[ids[:, 10]], tbl_11[ids[:, 11]], tbl_12[ids[:, 12]], tbl_13[ids[:, 13]], tbl_14[ids[:, 14]], tbl_15[ids[:, 15]], tbl_16[ids[:, 16]], tbl_17[ids[:, 17]], tbl_18[ids[:, 18]], tbl_19[ids[:, 19]], tbl_20[ids[:, 20]], tbl_21[ids[:, 21]], tbl_22[ids[:, 22]], tbl_23[ids[:, 23]], tbl_24[ids[:, 24]], tbl_25[ids[:, 25]]], axis=1)
    z = _L0_rec_ref(r_dense_t, e, L0_rec_Wd, L0_rec_gd, L0_rec_bd, L0_rec_Ws, L0_rec_gs, L0_rec_bs, L0_rec_Wsi, L0_rec_gsi, L0_rec_bsi, L0_rec_Wl, L0_rec_gl, L0_rec_bl, 384)
    z = z.reshape(z.shape[0], -1)
    h = jnp.concatenate([z, r_dense_t], axis=1)
    h = jnp.maximum(h @ W_top1 + b_top1, 0.0)
    h = jnp.maximum(h @ W_top2 + b_top2, 0.0)
    y = h @ W_top3
    return y

_drawn_inputs = setup_inputs


def setup_inputs(seed=0):
    import zlib

    import numpy as np

    out = dict(_drawn_inputs(seed))
    spreads = {'b_top1': (0.0, 0.1),
     'b_top2': (0.0, 0.1),
     'L0_rec_gd': (1.0, 0.6),
     'L0_rec_bd': (0.0, 0.8),
     'L0_rec_gs': (1.0, 0.6),
     'L0_rec_bs': (0.0, 0.1),
     'L0_rec_gsi': (1.0, 0.2),
     'L0_rec_bsi': (0.0, 0.1),
     'L0_rec_gl': (1.0, 0.2),
     'L0_rec_bl': (0.0, 0.1)}
    factors = {}
    for name, (base, spread) in spreads.items():
        noise = np.random.default_rng([zlib.crc32(name.encode()), seed]).standard_normal(out[name].shape)
        drawn = base * np.exp(spread * noise) if base else spread * noise
        out[name] = jnp.asarray(drawn.astype(out[name].dtype))
    for name, factor in factors.items():
        out[name] = (out[name] * factor).astype(out[name].dtype)
    return out
```

```python
from contextlib import ExitStack

import numpy as np

import concourse.bass as bass
from concourse import mybir

F32 = mybir.dt.float32
I32 = mybir.dt.int32
ALU = mybir.AluOpType
ACT = mybir.ActivationFunctionType
AX_X = mybir.AxisListType.X

P = 128
B = 2048
N_SP, D = 26, 64
D_DENSE = 256
E = 128
PROJ = 32
MAXD, USED = 512, 384
H1, H2 = 512, 256
EPS = 1e-5

TILE = 128
TILES = B // TILE
BLK = TILE // 2
CHUNKS = BLK * N_SP // P
GROUPS = [range(c, min(c + 4, CHUNKS)) for c in range(0, CHUNKS, 4)]
BANK = 512
SPB = BANK // PROJ
MIX_BANKS = BLK // SPB

QUAD = 4
OTHERS = QUAD + 1
ZCOLS = OTHERS + QUAD * PROJ
QUADS = TILE // QUAD
QPK = PROJ // 4
STEPS = QPK + 1
Y_PART = [0, 1, 2, 0]
ZBANKS = 4
ZBATCH = [3, 3, 2]
ZDVE = [1, 2, 1]


COLS = [("gd", 1), ("bd", 1), ("gsi_p", 1), ("bsi_p", 1), ("gsi_q", STEPS), ("bsi_q", STEPS), ("gl", 3), ("bl", 3),
        ("b1", 4), ("b2", 2)]


def chunk_windows():
    out, at = [], 0
    for c in range(CHUNKS):
        first, last = c * P // N_SP, (c * P + P - 1) // N_SP
        while first <= last:
            n = min(last + 1, (first // SPB + 1) * SPB) - first
            out.append((c, first, n, first // SPB, at))
            first += n
            at += n
    return out, at


WINDOWS, WIN_COLS = chunk_windows()


def tower(nc, io):
    with ExitStack() as ctx:
        def sb(name, shape, dt=F32):
            return ctx.enter_context(nc.sbuf_tensor(name, shape, dt))

        def sem(name):
            return ctx.enter_context(nc.semaphore(name))

        bank_a, bank_b, bank_c, bank_d = (
            ctx.enter_context(nc.psum_tensor(f"bank_{n}", [P, BANK], F32)) for n in "abcd")
        bank_z = ctx.enter_context(nc.psum_tensor("bank_z", [P, ZBANKS, BANK], F32))

        ident = sb("ident", [P, P])
        ones = sb("ones", [P, P])
        inv_e = sb("inv_e", [P, P])
        eps = sb("eps", [P, 1])
        ids_all = sb("ids_all", [P, TILES * 2 * CHUNKS], I32)
        row_base = sb("row_base", [P, 2 * CHUNKS], I32)
        ws_t = sb("ws_t", [P, E])
        gs_row = sb("gs_row", [P, E])
        ws_e = sb("ws_e", [P, P])
        gram = sb("gram", [P, P])
        proj_w = [sb("proj_w0", [P, E]), sb("proj_w1", [P, E])]
        wd_t = sb("wd_t", [P, 2, E])
        wsi_b = sb("wsi_b", [P, WIN_COLS, PROJ])
        wsi_n = sb("wsi_n", [N_SP, PROJ])
        bs_row = sb("bs_row", [N_SP, E])
        y_bias = sb("y_bias", [P, PROJ])
        wl = sb("wl", [P, STEPS, MAXD])
        fold_w = sb("fold_w", [P, STEPS, 65])
        mask_a = sb("mask_a", [P, 64])
        mask_b = sb("mask_b", [P, STEPS, 64])
        cols = sb("cols", [P, sum(n for _, n in COLS)])
        w1 = sb("w1", [P, 5, H1])
        w2 = sb("w2", [P, 4, H2])
        w3 = sb("w3", [P, 2])
        means = sb("means", [P, 160])
        b1 = sb("b1", [P, 4])
        col = {}
        at = 0
        for name, n in COLS:
            col[name] = cols[:, at:at + n]
            at += n

        dense_t = sb("dense_t", [P, 2, B])
        x_t = sb("x_t", [P, B])
        sum_x = sb("sum_x", [P, B])
        z_t = sb("z_t", [P, 3, B])

        ids = [sb(f"ids{i}", [P, 2 * CHUNKS], I32) for i in range(2)]
        rows = [sb(f"rows{i}", [P, CHUNKS, 2 * D]) for i in range(2)]
        rows_t = sb("rows_t", [P, CHUNKS, P])
        scaled = sb("scaled", [P, CHUNKS, 2 * D])
        row_var = sb("row_var", [P, 2 * CHUNKS])
        row_std = sb("row_std", [P, 2 * CHUNKS])
        row_r = sb("row_r", [P, 2 * CHUNKS])
        mixed = sb("mixed", [P, 2, BANK])
        y = sb("y", [P, 3, 2, BANK])
        y_sq = sb("y_sq", [P, 2, 2, BANK])
        y_var = sb("y_var", [P, MIX_BANKS, 2 * SPB])
        y_std = sb("y_std", [P, MIX_BANKS, 2 * SPB])
        y_r = sb("y_r", [P, MIX_BANKS, 2 * SPB])
        r_vec = sb("r_vec", [P, QUADS, ZCOLS])
        zd = [sb(f"zd{i}", [P, STEPS, TILE]) for i in range(2)]
        l_sq = sb("l_sq", [P, MAXD])
        l_var = sb("l_var", [P, 1])
        l_std = sb("l_std", [P, 1])
        l_r = sb("l_r", [P, 1])
        z_row = sb("z_row", [P, USED])
        h1 = y[:, 0:2, :, :].rearrange("p a b n -> p (a b) n")
        h2 = y_sq[:, 0, :, :]
        out_row = sum_x[0:1, :]

        s_ids, s_small, s_wsi, s_wl, s_dense, s_top = (
            sem(n) for n in ("ids_loaded", "small_loaded", "wsi_loaded", "wl_loaded", "dense_loaded", "top_loaded"))
        gathered = [sem("gathered_even"), sem("gathered_odd")]
        ids_ready = sem("ids_ready")
        ids_seen = sem("ids_seen")
        prep = sem("prep")
        pe_prep = sem("pe_prep")
        act_prep = sem("act_prep")
        turned = sem("turned")
        turned_kept = sem("turned_kept")
        gram_done = sem("gram_done")
        quad_done = sem("quad_done")
        var_done = sem("var_done")
        rstd_done = sem("rstd_done")
        rows_scaled = sem("rows_scaled")
        row_std_done = sem("row_std_done")
        mix_done = sem("mix_done")
        mix_kept = sem("mix_kept")
        y_done = sem("y_done")
        y_kept = sem("y_kept")
        y_squared = sem("y_squared")
        y_var_done = sem("y_var_done")
        y_std_done = sem("y_std_done")
        y_r_done = sem("y_r_done")
        r_ready = sem("r_ready")
        x_placed = sem("x_placed")
        z_done = sem("z_done")
        z_kept_act = sem("z_kept_act")
        z_kept_dve = sem("z_kept_dve")
        sumx_placed = sem("sumx_placed")
        l_done = sem("l_done")
        l_var_done = sem("l_var_done")
        l_std_done = sem("l_std_done")
        l_r_done = sem("l_r_done")
        z_scaled = sem("z_scaled")
        z_turned = sem("z_turned")
        z_kept = sem("z_kept")
        h1_done, h1_kept, h2_done, h2_kept, out_done, out_kept = (
            sem(n) for n in ("h1_done", "h1_kept", "h2_done", "h2_kept", "out_done", "out_kept"))
        stored = sem("stored")

        bank_t = [bank_a, bank_d]
        bank_g = [bank_b, bank_c]

        def z_moves(batch):
            per_bank = ZBATCH[batch]
            first = sum(ZBATCH[:batch]) * ZBANKS * QUAD
            n = per_bank * ZBANKS * QUAD
            out = []
            for j in range(QUAD):
                src = bank_z[PROJ * j:PROJ * (j + 1), :, 0:per_bank * ZCOLS]
                src = src.rearrange("p n (g c) -> p n g c", c=ZCOLS)

                def to(par, k, t0, t1, j=j):
                    v = zd[par][PROJ * k:PROJ * (k + 1), t0:t1, first:first + n]
                    return v.rearrange("p t (n g j) -> p n g j t", n=ZBANKS, j=QUAD)[:, :, :, j, :]

                for k in range(4):
                    c = OTHERS + PROJ * j + QPK * k
                    out.append((lambda par, k=k, to=to: to(par, k, 0, QPK), src[:, :, :, c:c + QPK]))
                out.append((lambda par, to=to: to(par, 0, QPK, STEPS), src[:, :, :, j:j + 1]))
                out.append((lambda par, to=to: to(par, 3, QPK, STEPS), src[:, :, :, QUAD:QUAD + 1]))
            cut = 6 * (QUAD - ZDVE[batch])
            return out[:cut], out[cut:]

        prep_at = {}

        block = ctx.enter_context(nc.Block())

        def over_tiles(eng, body):
            body(0, 0, True, False, False)
            body(1, 1, True, True, False)
            body(2, 0, True, True, True)
            body(3, 1, True, True, True)
            with eng.Fori(2, TILES // 2) as i:
                body(i * 2, 0, True, True, True)
                body(i * 2 + 1, 1, True, True, True)
            body(TILES, 0, False, True, True)
            body(TILES + 1, 1, False, False, True)

        @block.vector
        def _(dve):
            count = [0]

            def step(ins, name=None):
                count[0] += 1
                ins.then_inc(prep, 1)
                if name:
                    assert name not in prep_at
                    prep_at[name] = count[0]
                dve.wait_ge(prep, count[0])

            v = nc.vector
            step(v.memset(eps[:], EPS))
            step(v.memset(ones[:], 1.0))
            step(v.memset(inv_e[:], 1.0 / E), "constants")
            dve.wait_ge(s_small, 16 * 7)
            step(v.tensor_reduce(means[:, 0:1], ws_t[:], AX_X, ALU.add))
            step(v.tensor_scalar(means[:, 0:1], means[:, 0:1], -1.0 / E, None, ALU.mult))
            step(v.tensor_scalar(ws_t[:], ws_t[:], means[:, 0:1], None, ALU.add), "ws_centred")
            step(v.memset(proj_w[0][:], 0.0))
            step(v.memset(proj_w[1][:], 0.0))
            step(v.memset(gram[:], 0.0))
            for blk in range(2):
                half = slice(blk * D, (blk + 1) * D)
                step(v.tensor_tensor(proj_w[blk][half, :], ws_t[half, :], gs_row[half, :], ALU.mult))
            dve.wait_ge(pe_prep, 1)
            step(v.tensor_copy(ws_e[:], bank_a[:, 0:P]), "ws_e")
            step(v.tensor_reduce(means[0:N_SP, 0:1], wsi_n[:], AX_X, ALU.add))
            step(v.tensor_scalar(means[0:N_SP, 0:1], means[0:N_SP, 0:1], -1.0 / PROJ, None, ALU.mult))
            step(v.tensor_scalar(wsi_n[:], wsi_n[:], means[0:N_SP, 0:1], None, ALU.add), "wsi_n")
            step(v.tensor_reduce(means[:, 0:2], wd_t[:], AX_X, ALU.add))
            step(v.tensor_scalar(means[:, 0:2], means[:, 0:2], -1.0 / E, None, ALU.mult))
            for i in range(2):
                step(v.tensor_scalar(wd_t[:, i, :], wd_t[:, i, :], means[:, i:i + 1], None, ALU.add),
                     "wd_centred" if i else None)
            dve.wait_ge(pe_prep, 2)
            for blk in range(2):
                half = slice(blk * D, (blk + 1) * D)
                step(v.tensor_scalar(gram[half, half], bank_b[half, half], 1.0 / E, None, ALU.mult),
                     "gram" if blk else None)
            dve.wait_ge(pe_prep, 3)
            step(v.tensor_copy(y_bias[:], bank_c[:, 0:PROJ]), "y_bias")
            for j in range(B // BANK):
                cut = slice(j * BANK, (j + 1) * BANK)
                dve.wait_ge(act_prep, 2 + 3 * j)
                step(v.reciprocal(y_sq[:, 1, 0, :], y_sq[:, 0, 0, :]))
                step(v.tensor_tensor(x_t[:, cut], bank_a[:], y_sq[:, 1, 0, :], ALU.mult))
                step(v.tensor_scalar(x_t[:, cut], x_t[:, cut], col["gd"], col["bd"], ALU.mult, ALU.add), f"x{j}")
            dve.wait_ge(s_wsi, 16)
            m = means[:, 0:WIN_COLS]
            step(v.tensor_reduce(m, wsi_b[:], AX_X, ALU.add))
            step(v.tensor_scalar(m, m, -1.0 / PROJ, None, ALU.mult))
            step(v.tensor_tensor(wsi_b[:], wsi_b[:],
                                 m.rearrange("p (w o) -> p w o", o=1).broadcast_to([P, WIN_COLS, PROJ]), ALU.add))
            dve.wait_ge(s_wl, 16 * 3)
            bq = col["bsi_q"].rearrange("p (t o) -> p t o", o=1)
            fw = fold_w[:, :, 0:64]
            step(v.tensor_tensor(fw, mask_a[:].rearrange("p (o n) -> p o n", o=1).broadcast_to([P, STEPS, 64]),
                                 bq.broadcast_to([P, STEPS, 64]), ALU.mult))
            step(v.scalar_tensor_tensor(out=fw, in0=mask_b[:], scalar=col["bsi_p"], in1=fw, op0=ALU.mult, op1=ALU.add))
            step(v.tensor_scalar(fold_w[:, :, 64:65], bq, col["bsi_p"], float(E), ALU.mult, ALU.mult), "fold_w")
            step(v.tensor_scalar(col["gsi_q"], col["gsi_q"], col["gsi_p"], None, ALU.mult))
            dve.wait_ge(pe_prep, 16)
            for t in range(STEPS):
                step(v.tensor_scalar(wl[:, t, :], wl[:, t, :], col["gsi_q"][:, t:t + 1], None, ALU.mult))
            step(v.tensor_scalar(wl[3 * PROJ:P, QPK, :], bank_d[0:PROJ, :], col["gsi_p"][0:PROJ, :], None, ALU.mult))
            step(v.tensor_copy(wl[32:33, STEPS - 1, :], bank_d[32:33, :]))
            step(v.tensor_copy(wl[64:65, STEPS - 1, :], bank_d[64:65, :]))
            m = means[:, 0:STEPS]
            step(v.tensor_reduce(m, wl[:], AX_X, ALU.add))
            step(v.tensor_scalar(m, m, -1.0 / MAXD, None, ALU.mult))
            for t in range(STEPS):
                step(v.tensor_scalar(wl[:, t, :], wl[:, t, :], m[:, t:t + 1], None, ALU.add))
            dve.wait_ge(pe_prep, 17)
            step(v.tensor_tensor(b1[:], bank_z[:, 0, 0:4], col["b1"], ALU.add))
            for c in range(3):
                step(v.tensor_scalar(w1[:, c, :], w1[:, c, :], col["gl"][:, c:c + 1], None, ALU.mult))
            step(v.memset(r_vec[:, :, QUAD:OTHERS], 1.0))
            for i in range(2):
                step(v.memset(zd[i][:, STEPS - 1, :], 0.0))
                step(v.memset(zd[i][64:65, STEPS - 1, :], 1.0), "end" if i else None)

            def tile_work(t, par, load, inter, top):
                def keep_z(batch):
                    dve.wait_ge(z_done, 3 * (t - 1) + batch + 1)
                    for to, src in z_moves(batch)[1]:
                        ins = v.tensor_copy(to(1 - par), src)
                    ins.then_inc(z_kept_dve, 1)

                def keep_y(j):
                    for blk in range(2):
                        dve.wait_ge(y_done, 8 * t + 2 * j + blk + 1)
                        if j == 3:
                            dve.wait_ge(y_squared, 4 * t + 1)
                            dve.wait_ge(r_ready, 4 * t + 1)
                        elif inter:
                            dve.wait_ge(y_squared, 4 * t)
                            dve.wait_ge(r_ready, 4 * t)
                        v.tensor_tensor(
                            y[:, Y_PART[j], blk, :].rearrange("e (s p) -> e s p", p=PROJ),
                            bank_g[blk][:].rearrange("e (s p) -> e s p", p=PROJ),
                            y_bias[:].rearrange("e (o p) -> e o p", o=1).broadcast_to([P, SPB, PROJ]),
                            ALU.add).then_inc(y_kept, 1)

                def y_mean_square(j):
                    dve.wait_ge(y_squared, 4 * t + j + 1)
                    if inter:
                        dve.wait_ge(y_std_done, 4 * (t - 1) + j + 1)
                    v.tensor_reduce(y_var[:, j, :], y_sq[:, j % 2, :, :].rearrange("e a (s p) -> e (a s) p", p=PROJ),
                                    AX_X, ALU.add).then_inc(y_var_done, 1)

                def y_scale(j):
                    dve.wait_ge(y_std_done, 4 * t + j + 1)
                    if inter:
                        dve.wait_ge(r_ready, 4 * (t - 1) + j + 1)
                    v.reciprocal(y_r[:, j, :], y_std[:, j, :]).then_inc(y_r_done, 1)
                    dve.wait_ge(y_r_done, 4 * t + j + 1)
                    if inter:
                        dve.wait_ge(z_done, 3 * t)
                    for blk in range(2):
                        quad = blk * (QUADS // 2) + j * (SPB // QUAD)
                        ins = v.tensor_tensor(
                            r_vec[:, quad:quad + SPB // QUAD, OTHERS:ZCOLS].rearrange("e g (s p) -> e g s p", p=PROJ),
                            y[:, Y_PART[j], blk, :].rearrange("e (g s p) -> e g s p", g=SPB // QUAD, p=PROJ),
                            y_r[:, j, blk * SPB:(blk + 1) * SPB].rearrange("e (g s o) -> e g s o", s=QUAD, o=1)
                            .broadcast_to([P, SPB // QUAD, QUAD, PROJ]), ALU.mult)
                    ins.then_inc(r_ready, 1)

                if load:
                    for g in range(len(GROUPS)):
                        dve.wait_ge(gram_done, 4 * t + g + 1)
                        if inter:
                            dve.wait_ge(mix_done, 4 * t)
                        a, b = GROUPS[g][0], GROUPS[g][-1] + 1
                        v.tensor_tensor(scaled[:, a:b, :],
                                        bank_g[g % 2][:, 0:(b - a) * P].rearrange("p (c n) -> p c n", n=P),
                                        rows[par][:, a:b, :], ALU.mult).then_inc(quad_done, 1)
                    dve.wait_ge(quad_done, 4 * (t + 1))
                    if inter:
                        dve.wait_ge(row_std_done, t)
                    v.tensor_reduce(row_var[:], scaled[:].rearrange("p c (a d) -> p (c a) d", d=D), AX_X, ALU.add)\
                        .then_inc(var_done, 1)
                    dve.wait_ge(row_std_done, t + 1)
                    if inter:
                        dve.wait_ge(rows_scaled, 4 * t)
                    v.reciprocal(row_r[:], row_std[:]).then_inc(rstd_done, 1)
                    dve.wait_ge(rstd_done, t + 1)
                    dve.wait_ge(var_done, t + 1)
                    for g in range(len(GROUPS)):
                        a, b = GROUPS[g][0], GROUPS[g][-1] + 1
                        v.tensor_tensor(scaled[:, a:b, :].rearrange("p c (a d) -> p (c a) d", d=D),
                                        rows[par][:, a:b, :].rearrange("p c (a d) -> p (c a) d", d=D),
                                        row_r[:, 2 * a:2 * b].rearrange("p (n o) -> p n o", o=1)
                                        .broadcast_to([P, 2 * (b - a), D]), ALU.mult).then_inc(rows_scaled, 1)
                if inter:
                    if top:
                        dve.wait_ge(l_done, t - 2)
                    keep_z(0)
                    keep_z(1)
                if top:
                    dve.wait_ge(l_std_done, t - 1)
                    if top:
                        dve.wait_ge(z_scaled, t - 2)
                    v.reciprocal(l_r[:], l_std[:]).then_inc(l_r_done, 1)
                if inter:
                    keep_z(2)
                if load:
                    keep_y(0)
                    keep_y(1)
                    y_mean_square(0)
                    y_scale(0)
                    y_mean_square(1)
                    keep_y(2)
                    y_scale(1)
                    y_mean_square(2)
                    keep_y(3)
                    y_scale(2)
                    y_mean_square(3)
                    y_scale(3)

            over_tiles(dve, tile_work)

            with dve.Fori(0, B // BANK) as q:
                dve.wait_ge(out_done, q + 1)
                v.tensor_copy(out_row[:, bass.ds(q * BANK, BANK)], bank_a[0:1, :]).then_inc(out_kept, 1)

        @block.sync
        def _(sp):
            for dst, src in ((ids_all, "ids"), (row_base, "row_base")):
                sp.dma_start(dst[:], io[src]).then_inc(s_ids, 16)
            for dst, src in ((ws_t, "ws_t"), (gs_row, "gs_row"), (ident, "ident"), (cols, "cols"),
                             (wd_t, "wd_t"), (wsi_n, "wsi_n"), (bs_row, "bs_row")):
                sp.dma_start(dst[:], io[src]).then_inc(s_small, 16)
            sp.dma_start(dense_t[:], io["dense_t"]).then_inc(s_dense, 16)
            sp.dma_start(wsi_b[:], io["wsi_b"]).then_inc(s_wsi, 16)
            for dst, src in ((wl, "wl"), (mask_a, "mask_a"), (mask_b, "mask_b")):
                sp.dma_start(dst[:], io[src]).then_inc(s_wl, 16)
            for dst, src in ((w1, "w1"), (w2, "w2"), (w3, "w3")):
                sp.dma_start(dst[:], io[src]).then_inc(s_top, 16)
            sp.wait_ge(out_kept, B // BANK)
            sp.dma_start(io["out"].rearrange("b o -> o b"), out_row).then_inc(stored, 16)
            sp.wait_ge(stored, 16)

        @block.gpsimd
        def _(pool):
            pool.wait_ge(s_ids, 32)

            def gather(t, par, load, inter, top):
                if not load:
                    return
                if top:
                    pool.wait_ge(rows_scaled, len(GROUPS) * (t - 1))
                if top:
                    pool.wait_ge(gathered[par], (t - par) * (16 * CHUNKS))
                nc.gpsimd.tensor_tensor(ids[par][:], ids_all[:, bass.ds(t * (2 * CHUNKS), 2 * CHUNKS)],
                                        row_base[:], ALU.add).then_inc(ids_ready, 1)
                pool.wait_ge(ids_ready, t + 1)
                pool.sem_inc(ids_seen, 1)
                for n in range(2 * CHUNKS):
                    c, blk = divmod(n, 2)
                    nc.gpsimd.indirect_dma_start(
                        rows[par][:, c, D * blk:D * (blk + 1)], None, io["table"],
                        bass.IndirectOffsetOnAxis(ap=ids[par][:, n:n + 1], axis=0)).then_inc(gathered[par], 16)

            over_tiles(pool, gather)

        @block.tensor
        def _(pe):
            pe.wait_ge(s_small, 16 * 7)
            pe.wait_ge(prep, prep_at["ws_centred"])
            pe.transpose(bank_a[:, 0:P], ws_t[:], ident[:]).then_inc(pe_prep, 1)
            pe.wait_ge(prep, prep_at["ws_e"])
            pe.matmul(bank_b[:, 0:P], ws_e[:], ws_e[:], start=True, stop=True).then_inc(pe_prep, 1)
            pe.wait_ge(prep, prep_at["wsi_n"])
            pe.matmul(bank_c[:, 0:PROJ], bs_row[:], wsi_n[:], start=True, stop=True).then_inc(pe_prep, 1)
            pe.wait_ge(s_dense, 16)
            pe.wait_ge(prep, prep_at["wd_centred"])
            for j in range(B // BANK):
                cut = slice(j * BANK, (j + 1) * BANK)
                if j == 0:
                    pe.wait_ge(prep, prep_at["ws_e"])
                else:
                    pe.wait_ge(prep, prep_at[f"x{j - 1}"])
                for i in range(2):
                    mm = pe.matmul(bank_a[:], wd_t[:, i, :], dense_t[:, i, cut], start=(i == 0), stop=(i == 1))
                mm.then_inc(pe_prep, 1)
                pe.wait_ge(act_prep, 1 + 3 * j)
                if j == 0:
                    pe.wait_ge(prep, prep_at["gram"])
                pe.matmul(bank_b[:], inv_e[:], l_sq[:], start=True, stop=True).then_inc(pe_prep, 1)
                pe.wait_ge(prep, prep_at[f"x{j}"])
                pe.wait_ge(prep, prep_at["y_bias"])
                if j:
                    pe.wait_ge(act_prep, 3 * j)
                pe.matmul(bank_c[:], ones[:], x_t[:, cut], start=True, stop=True).then_inc(pe_prep, 1)
            pe.wait_ge(prep, prep_at["fold_w"])
            for t in range(STEPS):
                mm = pe.matmul(bank_d[0:65, :], fold_w[:, t, :], wl[:, t, :], start=(t == 0), stop=(t == STEPS - 1))
            mm.then_inc(pe_prep, 1)
            pe.wait_ge(s_top, 16 * 3)
            for k in range(4):
                for c in range(3):
                    mm = pe.matmul(bank_z[:, 0, k:k + 1], w1[:, c, k * P:(k + 1) * P], col["bl"][:, c:c + 1],
                                   start=(c == 0), stop=(c == 2))
            mm.then_inc(pe_prep, 1)
            pe.wait_ge(prep, prep_at["end"])
            pe.wait_ge(act_prep, 3 * (B // BANK))

            def tile_work(t, par, load, inter, top):
                def turn(g):
                    if g >= 2:
                        pe.wait_ge(turned_kept, 4 * t + g - 1)
                    for n, c in enumerate(GROUPS[g]):
                        mm = pe.transpose(bank_t[g % 2][:, n * P:(n + 1) * P], rows[par][:, c, :], ident[:])
                    mm.then_inc(turned, 1)

                def gram_product(g):
                    pe.wait_ge(turned_kept, 4 * t + g + 1)
                    if g == 0 and inter:
                        pe.wait_ge(y_kept, 8 * t)
                    if g >= 2:
                        pe.wait_ge(quad_done, 4 * t + g - 1)
                    for n, c in enumerate(GROUPS[g]):
                        mm = pe.matmul(bank_g[g % 2][:, n * P:(n + 1) * P], rows_t[:, c, :], gram[:],
                                       start=True, stop=True)
                    mm.then_inc(gram_done, 1)

                def interact(batch):
                    if batch == 0:
                        pe.wait_ge(r_ready, 4 * t)
                        pe.wait_ge(x_placed, t)
                    if batch or top:
                        pe.wait_ge(z_kept_act, 3 * (t - 1) + batch)
                        pe.wait_ge(z_kept_dve, 3 * (t - 1) + batch)
                    per_bank = ZBATCH[batch]
                    first = sum(ZBATCH[:batch]) * ZBANKS
                    for n in range(per_bank * ZBANKS):
                        mm = pe.matmul(bank_z[:, n // per_bank, (n % per_bank) * ZCOLS:(n % per_bank + 1) * ZCOLS],
                                       r_vec[:, first + n, OTHERS:ZCOLS], r_vec[:, first + n, :], start=True, stop=True)
                    mm.then_inc(z_done, 1)

                def linear(steps):
                    if steps[0] == 0:
                        pe.wait_ge(z_kept_act, 3 * (t - 1))
                        pe.wait_ge(z_kept_dve, 3 * (t - 1))
                        pe.wait_ge(sumx_placed, t - 1)
                        if load:
                            pe.wait_ge(turned_kept, 4 * (t + 1))
                        else:
                            pe.wait_ge(z_kept, t - 2)
                    for s in steps:
                        mm = pe.matmul(bank_d[:], zd[par][:, s, :], wl[:, s, :], start=(s == 0), stop=(s == STEPS - 1))
                    if steps[-1] == STEPS - 1:
                        mm.then_inc(l_done, 1)

                def mix(j):
                    if j == 0:
                        pe.wait_ge(rows_scaled, 4 * (t + 1))
                    else:
                        pe.wait_ge(mix_kept, 4 * t + j)
                    wins = [w for w in WINDOWS if w[3] == j]
                    for n, (c, s0, k, _, w0) in enumerate(wins):
                        o = (s0 - j * SPB) * PROJ
                        mm = pe.matmul(bank_a[:, o:o + k * PROJ], scaled[:, c, :], wsi_b[:, w0:w0 + k, :],
                                       start=(n == 0), stop=(n == len(wins) - 1), skip_group_check=True)
                    mm.then_inc(mix_done, 1)

                def project(j):
                    pe.wait_ge(mix_kept, 4 * t + j + 1)
                    for blk in range(2):
                        if j == 0:
                            pe.wait_ge(quad_done, 4 * (t + 1))
                        else:
                            pe.wait_ge(y_kept, 8 * t + 2 * (j - 1) + blk + 1)
                        pe.matmul(bank_g[blk][:], proj_w[blk][:], mixed[:, j % 2, :], start=True, stop=True)\
                            .then_inc(y_done, 1)

                if load:
                    pe.wait_ge(gathered[par], (t - par + 2) * (16 * CHUNKS))
                    if inter:
                        pe.wait_ge(mix_kept, 4 * t)
                    turn(0)
                    if top:
                        pe.wait_ge(z_kept, t - 2)
                    turn(1)
                    gram_product(0)
                    turn(2)
                    gram_product(1)
                    turn(3)
                    gram_product(2)
                    gram_product(3)
                if inter:
                    interact(0)
                if top:
                    linear(range(0, 5))
                if inter:
                    interact(1)
                if top:
                    linear(range(5, STEPS))
                if load:
                    mix(0)
                if inter:
                    interact(2)
                if load:
                    mix(1)
                    project(0)
                    mix(2)
                    project(1)
                    mix(3)
                    project(2)
                if top:
                    pe.wait_ge(z_scaled, t - 1)
                    for c in range(3):
                        mm = pe.transpose(bank_d[:, c * P:(c + 1) * P], z_row[:, c * P:(c + 1) * P], ident[:])
                    mm.then_inc(z_turned, 1)
                if load:
                    project(3)

            over_tiles(pe, tile_work)

            pe.wait_ge(z_kept, TILES)
            def top_layers(q):
                cut = bass.ds(q * BANK, BANK)
                pe.wait_ge(h1_kept, q * 4)
                pe.wait_ge(h2_kept, q * 2)
                pe.wait_ge(out_kept, q)
                for k in range(4):
                    for c in range(5):
                        rhs = z_t[:, c, cut] if c < 3 else dense_t[:, c - 3, cut]
                        mm = pe.matmul(bank_z[:, k, :], w1[:, c, k * P:(k + 1) * P], rhs, start=(c == 0), stop=(c == 4))
                    mm.then_inc(h1_done, 1)
                pe.wait_ge(h1_kept, q * 4 + 4)
                for k in range(2):
                    for c in range(4):
                        mm = pe.matmul(bank_g[k][:], w2[:, c, k * P:(k + 1) * P], h1[:, c, :], start=(c == 0), stop=(c == 3))
                    mm.then_inc(h2_done, 1)
                pe.wait_ge(h2_kept, q * 2 + 2)
                for c in range(2):
                    mm = pe.matmul(bank_a[0:1, :], w3[:, c:c + 1], h2[:, c, :], start=(c == 0), stop=(c == 1))
                mm.then_inc(out_done, 1)

            top_layers(0)
            with pe.Fori(1, B // BANK) as q:
                top_layers(q)

        @block.scalar
        def _(act):
            act.wait_ge(prep, prep_at["constants"])
            for j in range(B // BANK):
                cut = slice(j * BANK, (j + 1) * BANK)
                act.wait_ge(pe_prep, 4 + 3 * j)
                nc.scalar.activation(l_sq[:], bank_a[:], ACT.Square).then_inc(act_prep, 1)
                act.wait_ge(pe_prep, 5 + 3 * j)
                if j:
                    act.wait_ge(prep, prep_at[f"x{j - 1}"])
                nc.scalar.activation(y_sq[:, 0, 0, :], bank_b[:], ACT.Sqrt, bias=eps[:]).then_inc(act_prep, 1)
                act.wait_ge(pe_prep, 6 + 3 * j)
                nc.scalar.copy(sum_x[PROJ:PROJ + 1, cut], bank_c[PROJ:PROJ + 1, :]).then_inc(act_prep, 1)
            act.wait_ge(prep, prep_at["end"])

            def tile_work(t, par, load, inter, top):
                def keep_z(batch):
                    act.wait_ge(z_done, 3 * (t - 1) + batch + 1)
                    if batch == 0 and top:
                        act.wait_ge(l_done, t - 2)
                    for to, src in z_moves(batch)[0]:
                        ins = nc.scalar.copy(to(1 - par), src)
                    ins.then_inc(z_kept_act, 1)

                def square(j):
                    act.wait_ge(y_kept, 8 * t + 2 * j + 2)
                    if j >= 2:
                        act.wait_ge(y_var_done, 4 * t + j - 1)
                    elif inter:
                        act.wait_ge(y_var_done, 4 * t + j - 1)
                    nc.scalar.activation(y_sq[:, j % 2, :, :], y[:, Y_PART[j], :, :], ACT.Square).then_inc(y_squared, 1)

                def y_root(j):
                    act.wait_ge(y_var_done, 4 * t + j + 1)
                    if inter:
                        act.wait_ge(y_r_done, 4 * (t - 1) + j + 1)
                    nc.scalar.activation(y_std[:, j, :], y_var[:, j, :], ACT.Sqrt, bias=eps[:], scale=1.0 / PROJ)\
                        .then_inc(y_std_done, 1)

                def keep_mix(j):
                    act.wait_ge(mix_done, 4 * t + j + 1)
                    if inter or j >= 2:
                        act.wait_ge(y_done, 8 * t + 2 * j - 2)
                    nc.scalar.copy(mixed[:, j % 2, :], bank_a[:]).then_inc(mix_kept, 1)

                if load:
                    for g in range(len(GROUPS)):
                        act.wait_ge(turned, 4 * t + g + 1)
                        if inter:
                            act.wait_ge(gram_done, 4 * (t - 1) + g + 1)
                        cs = GROUPS[g]
                        nc.scalar.copy(rows_t[:, cs[0]:cs[-1] + 1, :],
                                       bank_t[g % 2][:, 0:len(cs) * P].rearrange("p (c n) -> p c n", n=P))\
                            .then_inc(turned_kept, 1)
                    act.wait_ge(var_done, t + 1)
                    if inter:
                        act.wait_ge(rstd_done, t)
                    nc.scalar.activation(row_std[:], row_var[:], ACT.Sqrt, bias=eps[:]).then_inc(row_std_done, 1)
                if inter:
                    keep_z(0)
                    nc.scalar.copy(zd[1 - par][PROJ:PROJ + 1, STEPS - 1, :],
                                   sum_x[PROJ:PROJ + 1, bass.ds((t - 1) * TILE, TILE)]).then_inc(sumx_placed, 1)
                    keep_z(1)
                if top:
                    act.wait_ge(l_done, t - 1)
                    nc.scalar.activation(l_sq[:], bank_d[:], ACT.Square, accum_out=l_var[:]).then_inc(l_var_done, 1)
                    act.wait_ge(l_var_done, t - 1)
                    act.wait_ge(l_r_done, t - 2)
                    nc.scalar.activation(l_std[:], l_var[:], ACT.Sqrt, bias=eps[:], scale=1.0 / MAXD)\
                        .then_inc(l_std_done, 1)
                if load:
                    keep_mix(0)
                if inter:
                    keep_z(2)
                if load:
                    if inter:
                        act.wait_ge(z_done, 3 * t)
                    nc.scalar.copy(r_vec[:, :, 0:QUAD], x_t[:, bass.ds(t * TILE, TILE)].rearrange("p (g j) -> p g j", j=QUAD))\
                        .then_inc(x_placed, 1)
                    keep_mix(1)
                if top:
                    act.wait_ge(l_r_done, t - 1)
                    if top:
                        act.wait_ge(z_turned, t - 2)
                    nc.scalar.activation(z_row[:], bank_d[:, 0:USED], ACT.Copy, scale=l_r[:]).then_inc(z_scaled, 1)
                if load:
                    square(0)
                    keep_mix(2)
                    y_root(0)
                    square(1)
                    keep_mix(3)
                    y_root(1)
                    square(2)
                    y_root(2)
                if top:
                    act.wait_ge(z_turned, t - 1)
                    nc.scalar.copy(z_t[:, :, bass.ds((t - 2) * TILE, TILE)],
                                   bank_d[:, 0:USED].rearrange("p (c b) -> p c b", c=3)).then_inc(z_kept, 1)
                if load:
                    square(3)
                    y_root(3)

            over_tiles(act, tile_work)

            def top_layers(q):
                for k in range(4):
                    act.wait_ge(h1_done, q * 4 + k + 1)
                    act.wait_ge(h2_done, q * 2)
                    nc.scalar.activation(h1[:, k, :], bank_z[:, k, :], ACT.Relu, bias=b1[:, k:k + 1]).then_inc(h1_kept, 1)
                for k in range(2):
                    act.wait_ge(h2_done, q * 2 + k + 1)
                    if k == 0:
                        act.wait_ge(out_done, q)
                    nc.scalar.activation(h2[:, k, :], bank_g[k][:], ACT.Relu, bias=col["b2"][:, k:k + 1])\
                        .then_inc(h2_kept, 1)

            top_layers(0)
            with act.Fori(1, B // BANK) as q:
                top_layers(q)


def column(a, n=1):
    return np.asarray(a).reshape(n, P).T


def laid_out(x):
    f32 = np.float32
    tables = [np.asarray(x[f"tbl_{f}"]) for f in range(N_SP)]
    first_row = np.cumsum([0] + [t.shape[0] for t in tables])[:-1]
    feature = (np.arange(CHUNKS * P) % N_SP).reshape(CHUNKS, P)
    ids = np.asarray(x["ids"]).reshape(TILES, 2, CHUNKS, P).transpose(3, 0, 2, 1)
    wsi = np.asarray(x["L0_rec_Wsi"])
    wsi_b = np.zeros((P, WIN_COLS, PROJ), f32)
    for c, s0, k, _, w0 in WINDOWS:
        for r in range(P):
            s, n = divmod(c * P + r, N_SP)
            if s0 <= s < s0 + k:
                wsi_b[r, w0 + s - s0] = wsi[:, n]
    lin = np.asarray(x["L0_rec_Wl"])
    gsi, bsi = np.asarray(x["L0_rec_gsi"]), np.asarray(x["L0_rec_bsi"])
    wl = np.zeros((P, STEPS, MAXD), f32)
    gsi_q = np.ones((P, STEPS), f32)
    bsi_q = np.zeros((P, STEPS), f32)
    mask_a = np.zeros((P, 64), f32)
    mask_b = np.zeros((P, STEPS, 64), f32)
    for k in range(4):
        quarter = slice(PROJ * k, PROJ * (k + 1))
        mask_a[quarter, 0:PROJ] = np.eye(PROJ, dtype=f32)
        for t in range(QPK):
            q = QPK * k + t
            gsi_q[quarter, t] = gsi[q]
            bsi_q[quarter, t] = bsi[q]
            mask_b[quarter, t, q] = 1.0
            for p in range(q + 1, PROJ):
                wl[PROJ * k + p, t] = lin[:, (p + 1) * p // 2 + q + 1]
    for p in range(PROJ):
        wl[p, QPK] = lin[:, (p + 1) * p // 2]
    mask_b[0:PROJ, QPK, PROJ] = 1.0
    cols = {
        "gd": column(x["L0_rec_gd"]), "bd": column(x["L0_rec_bd"]),
        "gsi_p": np.tile(gsi, 4)[:, None], "bsi_p": np.tile(bsi, 4)[:, None],
        "gsi_q": gsi_q, "bsi_q": bsi_q,
        "gl": column(np.asarray(x["L0_rec_gl"])[:USED], 3), "bl": column(np.asarray(x["L0_rec_bl"])[:USED], 3),
        "b1": column(x["b_top1"], 4), "b2": column(x["b_top2"], 2),
    }
    top1 = np.asarray(x["W_top1"])
    top1 = np.concatenate([top1[:USED], top1[MAXD:]])
    dense_t = np.asarray(x["r_dense_t"]).T
    ws = np.asarray(x["L0_rec_Ws"])
    arrays = {
        "table": np.concatenate(tables),
        "ids": ids.reshape(P, -1),
        "row_base": np.repeat(first_row[feature].T, 2, axis=1).astype(np.int32),
        "ident": np.eye(P, dtype=f32),
        "ws_t": np.concatenate([ws.T, ws.T]),
        "gs_row": np.broadcast_to(np.asarray(x["L0_rec_gs"]), (P, E)),
        "bs_row": np.broadcast_to(np.asarray(x["L0_rec_bs"]), (N_SP, E)),
        "wsi_n": wsi.T, "wsi_b": wsi_b, "wl": wl, "mask_a": mask_a, "mask_b": mask_b,
        "wd_t": np.asarray(x["L0_rec_Wd"]).T.reshape(2, P, E).transpose(1, 0, 2),
        "dense_t": dense_t.reshape(2, P, B).transpose(1, 0, 2),
        "cols": np.concatenate([cols[name] for name, _ in COLS], axis=1),
        "w1": top1.reshape(5, P, H1).transpose(1, 0, 2),
        "w2": np.asarray(x["W_top2"]).reshape(4, P, H2).transpose(1, 0, 2),
        "w3": column(x["W_top3"], 2),
    }
    return {name: np.ascontiguousarray(a) for name, a in arrays.items()}


def kernel(**inputs):
    import concourse.bacc as bacc
    from concourse.bass_utils import run_bass_kernel_spmd

    nc = bacc.Bacc("TRN2", target_bir_lowering=False, num_devices=1)
    arrays = laid_out(inputs)
    io = {name: nc.dram_tensor(f"in_{name}", a.shape, mybir.dt.from_np(a.dtype), kind="ExternalInput").ap()
          for name, a in arrays.items()}
    io["out"] = nc.dram_tensor("out", (B, 1), F32, kind="ExternalOutput").ap()
    tower(nc, io)
    r = run_bass_kernel_spmd(nc, [{f"in_{name}": a for name, a in arrays.items()}], core_ids=[0])
    return r.results[0]["out"]
```

```python
from contextlib import ExitStack

import numpy as np

import concourse.bass as bass
from concourse import mybir

F32 = mybir.dt.float32
F32R = mybir.dt.float32r
I32 = mybir.dt.int32
ALU = mybir.AluOpType
ACT = mybir.ActivationFunctionType
AX_X = mybir.AxisListType.X

P = 128
B = 2048
N_SP, D = 26, 64
D_DENSE = 256
E = 128
PROJ = 32
MAXD, USED = 512, 384
H1, H2 = 512, 256
EPS = 1e-5

TILE = 128
TILES = B // TILE
BLK = TILE // 2
CHUNKS = BLK * N_SP // P
GROUPS = [range(c, min(c + 4, CHUNKS)) for c in range(0, CHUNKS, 4)]
BANK = 512
SPB = BANK // PROJ
MIX_BANKS = BLK // SPB

QUAD = 4
OTHERS = QUAD + 1
ZCOLS = OTHERS + QUAD * PROJ
QUADS = TILE // QUAD
QPK = PROJ // 4
STEPS = QPK + 1
Y_PART = [0, 1, 2, 0]
ZBANKS = 4
ZBATCH = [3, 3, 2]
ZDVE = [1, 1, 1]
ZDVE_TILE = sum(n > 0 for n in ZDVE)


COLS = [("gd", 1), ("bd", 1), ("gsi_p", 1), ("bsi_p", 1), ("gsi_q", STEPS), ("bsi_q", STEPS), ("gl", 3), ("bl", 3),
        ("b1", 4), ("b2", 2)]


def chunk_windows():
    out, at = [], 0
    for c in range(CHUNKS):
        first, last = c * P // N_SP, (c * P + P - 1) // N_SP
        while first <= last:
            bank = first // SPB
            end = min(last + 1, (bank + 1) * SPB)
            n = max(end - first, 3)
            start = min(first, (bank + 1) * SPB - n)
            out.append((c, start, n, bank, at))
            at += n
            first = end
    return out, at


WINDOWS, WIN_COLS = chunk_windows()


def tower(nc, io):
    with ExitStack() as ctx:
        def sb(name, shape, dt=F32):
            return ctx.enter_context(nc.sbuf_tensor(name, shape, dt))

        def sem(name):
            return ctx.enter_context(nc.semaphore(name))

        bank_a, bank_b, bank_c, bank_d = (
            ctx.enter_context(nc.psum_tensor(f"bank_{n}", [P, BANK], F32)) for n in "abcd")
        bank_z = ctx.enter_context(nc.psum_tensor("bank_z", [P, ZBANKS, BANK], F32))

        ident = sb("ident", [P, P])
        ones = sb("ones", [P, P])
        eps = sb("eps", [P, 1])
        ids_all = sb("ids_all", [P, TILES * 2 * CHUNKS], I32)
        row_base = sb("row_base", [P, 2 * CHUNKS], I32)
        ws_t = sb("ws_t", [P, E])
        gs_row = sb("gs_row", [P, E])
        ws_e = sb("ws_e", [P, P])
        gram = sb("gram", [P, P])
        proj_hi = sb("proj_hi", [P, E], F32R)
        proj_lo = sb("proj_lo", [P, E], F32R)
        wd_t = sb("wd_t", [P, 2, E])
        wsi_b = sb("wsi_b", [P, WIN_COLS, PROJ])
        wsi_n = sb("wsi_n", [N_SP, PROJ])
        bs_row = sb("bs_row", [N_SP, E])
        y_bias = sb("y_bias", [P, PROJ])
        wl = sb("wl", [P, STEPS, MAXD])
        fold_w = sb("fold_w", [P, STEPS, 65])
        mask_a = sb("mask_a", [P, 64])
        mask_b = sb("mask_b", [P, STEPS, 64])
        cols = sb("cols", [P, sum(n for _, n in COLS)])
        w1 = sb("w1", [P, 5, H1])
        w2 = sb("w2", [P, 4, H2])
        w3 = sb("w3", [P, 2])
        means = sb("means", [P, 160])
        b1 = sb("b1", [P, 4])
        col = {}
        at = 0
        for name, n in COLS:
            col[name] = cols[:, at:at + n]
            at += n

        dense_t = sb("dense_t", [P, 2, B])
        x_t = sb("x_t", [P, B])
        sum_x = sb("sum_x", [P, B])

        ids = [sb(f"ids{i}", [P, 2 * CHUNKS], I32) for i in range(2)]
        rows = [sb(f"rows{i}", [P, CHUNKS, 2 * D]) for i in range(2)]
        rows_t = sb("rows_t", [P, CHUNKS, P])
        scaled = sb("scaled", [P, CHUNKS, 2 * D])
        row_var = sb("row_var", [P, 2 * CHUNKS])
        row_std = sb("row_std", [P, 2 * CHUNKS])
        row_r = sb("row_r", [P, 2 * CHUNKS])
        mixed = sb("mixed", [P, 2, 2, BANK], F32R)
        y = sb("y", [P, 3, 2, BANK])
        y_sq = sb("y_sq", [P, 2, 2, BANK])
        y_var = sb("y_var", [P, MIX_BANKS, 2 * SPB])
        y_std = sb("y_std", [P, MIX_BANKS, 2 * SPB])
        y_r = sb("y_r", [P, MIX_BANKS, 2 * SPB])
        r_vec = sb("r_vec", [P, QUADS, ZCOLS])
        zd = sb("zd", [P, STEPS, TILE])
        l_sq = sb("l_sq", [P, MAXD])
        l_var = sb("l_var", [P, 1])
        l_std = sb("l_std", [P, 1])
        l_r = sb("l_r", [P, 1])
        z_row = sb("z_row", [P, USED])
        z_t = sb("z_t", [P, 3, TILE])
        h1 = sb("h1", [P, 4, TILE])
        h2 = sb("h2", [P, 2, TILE])
        x_row = sb("x_row", [P, 4, E])
        x_var = sb("x_var", [P, TILES])
        x_std = sb("x_std", [P, TILES])
        x_r = sb("x_r", [P, TILES])
        out_row = sb("out_row", [1, B])

        s_ids, s_small, s_wsi, s_wl, s_dense, s_top = (
            sem(n) for n in ("ids_loaded", "small_loaded", "wsi_loaded", "wl_loaded", "dense_loaded", "top_loaded"))
        gathered = [sem("gathered_even"), sem("gathered_odd")]
        ids_ready = sem("ids_ready")
        ids_seen = sem("ids_seen")
        prep = sem("prep")
        pe_prep = sem("pe_prep")
        act_prep = sem("act_prep")
        x_squared = sem("x_squared")
        turned = sem("turned")
        turned_kept = sem("turned_kept")
        gram_done = sem("gram_done")
        quad_done = sem("quad_done")
        var_done = sem("var_done")
        rstd_done = sem("rstd_done")
        rows_scaled = sem("rows_scaled")
        row_std_done = sem("row_std_done")
        mix_done = sem("mix_done")
        mix_hi = sem("mix_hi")
        mix_lo = sem("mix_lo")
        y_done = sem("y_done")
        y_kept = sem("y_kept")
        y_squared = sem("y_squared")
        y_var_done = sem("y_var_done")
        y_std_done = sem("y_std_done")
        y_r_done = sem("y_r_done")
        r_ready = sem("r_ready")
        x_placed = sem("x_placed")
        z_done = sem("z_done")
        z_kept_act = sem("z_kept_act")
        z_kept_dve = sem("z_kept_dve")
        sumx_placed = sem("sumx_placed")
        l_done = sem("l_done")
        l_var_done = sem("l_var_done")
        l_std_done = sem("l_std_done")
        l_r_done = sem("l_r_done")
        z_scaled = sem("z_scaled")
        z_turned = sem("z_turned")
        z_kept = sem("z_kept")
        h1_done, h1_kept, h2_done, h2_kept, out_done, out_kept = (
            sem(n) for n in ("h1_done", "h1_kept", "h2_done", "h2_kept", "out_done", "out_kept"))
        stored = sem("stored")

        bank_g = [bank_b, bank_c]
        bank_m = [bank_a, bank_d]
        bank_l = bank_z[:, 3, :]
        bank_w = bank_z[:, 2, :]
        bank_t = [bank_z[:, i, :] for i in range(2)]

        def z_moves(batch):
            per_bank = ZBATCH[batch]
            first = sum(ZBATCH[:batch]) * ZBANKS * QUAD
            n = per_bank * ZBANKS * QUAD
            out = []
            for j in range(QUAD):
                src = bank_z[PROJ * j:PROJ * (j + 1), :, 0:per_bank * ZCOLS]
                src = src.rearrange("p n (g c) -> p n g c", c=ZCOLS)

                def to(k, t0, t1, j=j):
                    v = zd[PROJ * k:PROJ * (k + 1), t0:t1, first:first + n]
                    return v.rearrange("p t (n g j) -> p n g j t", n=ZBANKS, j=QUAD)[:, :, :, j, :]

                for k in range(4):
                    c = OTHERS + PROJ * j + QPK * k
                    out.append((to(k, 0, QPK), src[:, :, :, c:c + QPK]))
                out.append((to(0, QPK, STEPS), src[:, :, :, j:j + 1]))
                out.append((to(3, QPK, STEPS), src[:, :, :, QUAD:QUAD + 1]))
            cut = 6 * (QUAD - ZDVE[batch])
            return out[:cut], out[cut:]

        prep_at = {}

        block = ctx.enter_context(nc.Block())

        def over_tiles(eng, body, between=lambda: None):
            body(0, 0, True, True, False, False)
            between()
            body(1, 1, True, True, True, False)
            body(2, 0, True, True, True, True)
            body(3, 1, True, True, True, True)
            with eng.Fori(2, TILES // 2 - 1) as i:
                body(i * 2, 0, True, True, True, True)
                body(i * 2 + 1, 1, True, True, True, True)
            body(TILES - 2, 0, True, True, True, True)
            body(TILES - 1, 1, False, True, True, True)
            body(TILES, 0, False, False, True, True)
            body(TILES + 1, 1, False, False, False, True)

        @block.vector
        def _(dve):
            count = [0]

            def step(ins, name=None):
                count[0] += 1
                ins.then_inc(prep, 1)
                if name:
                    assert name not in prep_at
                    prep_at[name] = count[0]
                dve.wait_ge(prep, count[0])

            v = nc.vector
            step(v.memset(eps[:], EPS))
            step(v.memset(ones[:], 1.0), "constants")
            dve.wait_ge(s_small, 16 * 7)
            step(v.tensor_reduce(means[:, 0:1], ws_t[:], AX_X, ALU.add))
            step(v.tensor_scalar(means[:, 0:1], means[:, 0:1], -1.0 / E, None, ALU.mult))
            step(v.tensor_scalar(ws_t[:], ws_t[:], means[:, 0:1], None, ALU.add), "ws_centred")
            step(v.memset(gram[:], 0.0))
            step(v.tensor_tensor(gs_row[:], ws_t[:], gs_row[:], ALU.mult))
            step(v.tensor_copy(proj_hi[:], gs_row[:]))
            step(v.tensor_tensor(proj_lo[:], gs_row[:], proj_hi[:].bitcast(F32), ALU.subtract))
            dve.wait_ge(pe_prep, 1)
            step(v.tensor_copy(ws_e[:], bank_a[:, 0:P]), "ws_e")
            step(v.tensor_reduce(means[0:N_SP, 0:1], wsi_n[:], AX_X, ALU.add))
            step(v.tensor_scalar(means[0:N_SP, 0:1], means[0:N_SP, 0:1], -1.0 / PROJ, None, ALU.mult))
            step(v.tensor_scalar(wsi_n[:], wsi_n[:], means[0:N_SP, 0:1], None, ALU.add), "wsi_n")
            step(v.tensor_reduce(means[:, 0:2], wd_t[:], AX_X, ALU.add))
            step(v.tensor_scalar(means[:, 0:2], means[:, 0:2], -1.0 / E, None, ALU.mult))
            for i in range(2):
                step(v.tensor_scalar(wd_t[:, i, :], wd_t[:, i, :], means[:, i:i + 1], None, ALU.add),
                     "wd_centred" if i else None)
            dve.wait_ge(pe_prep, 2)
            for blk in range(2):
                half = slice(blk * D, (blk + 1) * D)
                step(v.tensor_scalar(gram[half, half], bank_b[half, half], 1.0 / E, None, ALU.mult),
                     "gram" if blk else None)
            dve.wait_ge(pe_prep, 3)
            step(v.tensor_copy(y_bias[:], bank_c[:, 0:PROJ]), "y_bias")
            for j in range(4):
                four = slice(4 * j, 4 * j + 4)
                dve.wait_ge(act_prep, j + 1)
                step(v.reciprocal(x_r[:, four], x_std[:, four]))
                if j:
                    dve.wait_ge(pe_prep, 3 + 4 + j)
                step(v.tensor_tensor(x_row[:], bank_z[:, j, :].rearrange("b (t e) -> b t e", t=4),
                                     x_r[:, four].rearrange("b (t o) -> b t o", o=1).broadcast_to([P, 4, E]),
                                     ALU.mult), f"x_row{j}")
                dve.wait_ge(pe_prep, 3 + 4 + j + 1)
                step(v.tensor_scalar(x_t[:, j * BANK:(j + 1) * BANK], bank_m[j % 2][:], col["gd"], col["bd"],
                                     ALU.mult, ALU.add), f"x{j}")
            dve.wait_ge(s_wsi, 16)
            m = means[:, 0:WIN_COLS]
            step(v.tensor_reduce(m, wsi_b[:], AX_X, ALU.add))
            step(v.tensor_scalar(m, m, -1.0 / PROJ, None, ALU.mult))
            step(v.tensor_tensor(wsi_b[:], wsi_b[:],
                                 m.rearrange("p (w o) -> p w o", o=1).broadcast_to([P, WIN_COLS, PROJ]), ALU.add))
            step(v.memset(r_vec[:, :, QUAD:OTHERS], 1.0))
            step(v.memset(zd[:, STEPS - 1, :], 0.0))
            step(v.memset(zd[64:65, STEPS - 1, :], 1.0), "end")

            def prepare_rest():
                dve.wait_ge(s_wl, 16 * 3)
                bq = col["bsi_q"].rearrange("p (t o) -> p t o", o=1)
                fw = fold_w[:, :, 0:64]
                step(v.tensor_tensor(fw, mask_a[:].rearrange("p (o n) -> p o n", o=1).broadcast_to([P, STEPS, 64]),
                                     bq.broadcast_to([P, STEPS, 64]), ALU.mult))
                step(v.scalar_tensor_tensor(out=fw, in0=mask_b[:], scalar=col["bsi_p"], in1=fw, op0=ALU.mult, op1=ALU.add))
                step(v.tensor_scalar(fold_w[:, :, 64:65], bq, col["bsi_p"], float(E), ALU.mult, ALU.mult), "fold_w")
                step(v.tensor_scalar(col["gsi_q"], col["gsi_q"], col["gsi_p"], None, ALU.mult))
                dve.wait_ge(pe_prep, 16)
                for t in range(STEPS):
                    step(v.tensor_scalar(wl[:, t, :], wl[:, t, :], col["gsi_q"][:, t:t + 1], None, ALU.mult))
                step(v.tensor_scalar(wl[3 * PROJ:P, QPK, :], bank_d[0:PROJ, :], col["gsi_p"][0:PROJ, :], None, ALU.mult))
                step(v.tensor_copy(wl[32:33, STEPS - 1, :], bank_d[32:33, :]))
                step(v.tensor_copy(wl[64:65, STEPS - 1, :], bank_d[64:65, :]))
                m = means[:, 0:STEPS]
                step(v.tensor_reduce(m, wl[:], AX_X, ALU.add))
                step(v.tensor_scalar(m, m, -1.0 / MAXD, None, ALU.mult))
                for t in range(STEPS):
                    step(v.tensor_scalar(wl[:, t, :], wl[:, t, :], m[:, t:t + 1], None, ALU.add))
                dve.wait_ge(pe_prep, 17)
                step(v.tensor_tensor(b1[:], bank_a[:, 0:4], col["b1"], ALU.add))
                for c in range(3):
                    step(v.tensor_scalar(w1[:, c, :], w1[:, c, :], col["gl"][:, c:c + 1], None, ALU.mult),
                         "rest" if c == 2 else None)

            def tile_work(t, par, more, load, inter, top):
                def keep_z(batch):
                    if not ZDVE[batch]:
                        return
                    dve.wait_ge(z_done, 3 * (t - 1) + batch + 1)
                    if batch == 0 and top:
                        dve.wait_ge(l_done, t - 1)
                    for to, src in z_moves(batch)[1]:
                        ins = v.tensor_copy(to, src)
                    ins.then_inc(z_kept_dve, 1)

                def keep_low(j):
                    for blk in range(2):
                        own, other = slice(D * blk, D * (blk + 1)), slice(D * (1 - blk), D * (2 - blk))
                        dve.wait_ge(mix_hi, 8 * t + 2 * j + blk + 1)
                        if inter or j >= 2:
                            dve.wait_ge(y_done, 8 * t + 2 * j + blk - 3)
                        v.tensor_tensor(mixed[other, j % 2, blk, :], bank_m[j % 2][own, :],
                                        mixed[own, j % 2, blk, :].bitcast(F32), ALU.subtract).then_inc(mix_lo, 1)

                def keep_y(j):
                    for blk in range(2):
                        dve.wait_ge(y_done, 8 * t + 2 * j + blk + 1)
                        if j == 3:
                            dve.wait_ge(y_squared, 8 * t + blk + 1)
                            dve.wait_ge(r_ready, 4 * t + 1)
                        elif inter:
                            dve.wait_ge(y_squared, 8 * t)
                            dve.wait_ge(r_ready, 4 * t)
                        v.tensor_tensor(
                            y[:, Y_PART[j], blk, :].rearrange("e (s p) -> e s p", p=PROJ),
                            bank_g[blk][:].rearrange("e (s p) -> e s p", p=PROJ),
                            y_bias[:].rearrange("e (o p) -> e o p", o=1).broadcast_to([P, SPB, PROJ]),
                            ALU.add).then_inc(y_kept, 1)

                def y_mean_square(j):
                    dve.wait_ge(y_squared, 8 * t + 2 * j + 2)
                    if inter:
                        dve.wait_ge(y_std_done, 4 * (t - 1) + j + 1)
                    v.tensor_reduce(y_var[:, j, :], y_sq[:, j % 2, :, :].rearrange("e a (s p) -> e (a s) p", p=PROJ),
                                    AX_X, ALU.add).then_inc(y_var_done, 1)

                def y_scale(t, j, inter):
                    dve.wait_ge(y_std_done, 4 * t + j + 1)
                    if inter:
                        dve.wait_ge(r_ready, 4 * (t - 1) + j + 1)
                    v.reciprocal(y_r[:, j, :], y_std[:, j, :]).then_inc(y_r_done, 1)
                    dve.wait_ge(y_r_done, 4 * t + j + 1)
                    if inter:
                        dve.wait_ge(z_done, 3 * t)
                    for blk in range(2):
                        quad = (2 * j + blk) * (SPB // QUAD)
                        ins = v.tensor_tensor(
                            r_vec[:, quad:quad + SPB // QUAD, OTHERS:ZCOLS].rearrange("e g (s p) -> e g s p", p=PROJ),
                            y[:, Y_PART[j], blk, :].rearrange("e (g s p) -> e g s p", g=SPB // QUAD, p=PROJ),
                            y_r[:, j, blk * SPB:(blk + 1) * SPB].rearrange("e (g s o) -> e g s o", s=QUAD, o=1)
                            .broadcast_to([P, SPB // QUAD, QUAD, PROJ]), ALU.mult)
                    ins.then_inc(r_ready, 1)

                def square_form(g):
                    dve.wait_ge(gram_done, 4 * t + g + 1)
                    if inter:
                        dve.wait_ge(mix_done, 4 * t)
                    a, b = GROUPS[g][0], GROUPS[g][-1] + 1
                    v.tensor_tensor(scaled[:, a:b, :],
                                    bank_g[g % 2][:, 0:(b - a) * P].rearrange("p (c n) -> p c n", n=P),
                                    rows[par][:, a:b, :], ALU.mult).then_inc(quad_done, 1)

                def row_mean_square():
                    dve.wait_ge(quad_done, 4 * (t + 1))
                    if inter:
                        dve.wait_ge(row_std_done, t)
                    v.tensor_reduce(row_var[:], scaled[:].rearrange("p c (a d) -> p (c a) d", d=D), AX_X, ALU.add)\
                        .then_inc(var_done, 1)

                def row_reciprocal():
                    dve.wait_ge(row_std_done, t + 1)
                    if inter:
                        dve.wait_ge(rows_scaled, 4 * t)
                    v.reciprocal(row_r[:], row_std[:]).then_inc(rstd_done, 1)
                    dve.wait_ge(rstd_done, t + 1)
                    dve.wait_ge(var_done, t + 1)

                def scale_rows(groups):
                    for g in groups:
                        a, b = GROUPS[g][0], GROUPS[g][-1] + 1
                        v.tensor_tensor(scaled[:, a:b, :].rearrange("p c (a d) -> p (c a) d", d=D),
                                        rows[par][:, a:b, :].rearrange("p c (a d) -> p (c a) d", d=D),
                                        row_r[:, 2 * a:2 * b].rearrange("p (n o) -> p n o", o=1)
                                        .broadcast_to([P, 2 * (b - a), D]), ALU.mult).then_inc(rows_scaled, 1)

                def linear_reciprocal():
                    dve.wait_ge(l_std_done, t)
                    if top:
                        dve.wait_ge(z_scaled, t - 1)
                    v.reciprocal(l_r[:], l_std[:]).then_inc(l_r_done, 1)

                if load:
                    square_form(0)
                    square_form(1)
                if inter:
                    y_scale(t - 1, 3, top)
                if load:
                    square_form(2)
                    square_form(3)
                    row_mean_square()
                    row_reciprocal()
                    scale_rows(range(len(GROUPS)))
                    keep_low(0)
                if inter:
                    keep_z(0)
                if load:
                    keep_y(0)
                    y_mean_square(0)
                if inter:
                    keep_z(1)
                if load:
                    keep_low(1)
                    keep_low(2)
                if inter:
                    keep_z(2)
                if load:
                    keep_y(1)
                    y_scale(t, 0, inter)
                    y_mean_square(1)
                    keep_low(3)
                    keep_y(2)
                    y_scale(t, 1, inter)
                    y_mean_square(2)
                    keep_y(3)
                    y_scale(t, 2, inter)
                if inter:
                    linear_reciprocal()
                if load:
                    y_mean_square(3)

            over_tiles(dve, tile_work, prepare_rest)

        @block.sync
        def _(sp):
            for dst, src in ((ids_all, "ids"), (row_base, "row_base")):
                sp.dma_start(dst[:], io[src]).then_inc(s_ids, 16)
            for dst, src in ((ws_t, "ws_t"), (gs_row, "gs_row"), (ident, "ident"), (cols, "cols"),
                             (wd_t, "wd_t"), (wsi_n, "wsi_n"), (bs_row, "bs_row")):
                sp.dma_start(dst[:], io[src]).then_inc(s_small, 16)
            sp.dma_start(dense_t[:], io["dense_t"]).then_inc(s_dense, 16)
            sp.dma_start(wsi_b[:], io["wsi_b"]).then_inc(s_wsi, 16)
            for dst, src in ((wl, "wl"), (mask_a, "mask_a"), (mask_b, "mask_b")):
                sp.dma_start(dst[:], io[src]).then_inc(s_wl, 16)
            for dst, src in ((w1, "w1"), (w2, "w2"), (w3, "w3")):
                sp.dma_start(dst[:], io[src]).then_inc(s_top, 16)
            sp.wait_ge(out_kept, TILES)
            sp.dma_start(io["out"].rearrange("b o -> o b"), out_row[:]).then_inc(stored, 16)
            sp.wait_ge(stored, 16)

        @block.gpsimd
        def _(pool):
            pool.wait_ge(s_ids, 32)

            def gather(t, par, more, load, inter, top):
                if not load:
                    return
                if top:
                    pool.wait_ge(rows_scaled, len(GROUPS) * (t - 1))
                if top:
                    pool.wait_ge(gathered[par], (t - par) * (16 * CHUNKS))
                nc.gpsimd.tensor_tensor(ids[par][:], ids_all[:, bass.ds(t * (2 * CHUNKS), 2 * CHUNKS)],
                                        row_base[:], ALU.add).then_inc(ids_ready, 1)
                pool.wait_ge(ids_ready, t + 1)
                pool.sem_inc(ids_seen, 1)
                for n in range(2 * CHUNKS):
                    c, blk = divmod(n, 2)
                    nc.gpsimd.indirect_dma_start(
                        rows[par][:, c, D * blk:D * (blk + 1)], None, io["table"],
                        bass.IndirectOffsetOnAxis(ap=ids[par][:, n:n + 1], axis=0)).then_inc(gathered[par], 16)

            over_tiles(pool, gather)

        @block.tensor
        def _(pe):
            pe.wait_ge(s_small, 16 * 7)
            pe.wait_ge(prep, prep_at["ws_centred"])
            pe.transpose(bank_a[:, 0:P], ws_t[:], ident[:]).then_inc(pe_prep, 1)
            pe.wait_ge(prep, prep_at["ws_e"])
            pe.matmul(bank_b[:, 0:P], ws_e[:], ws_e[:], start=True, stop=True).then_inc(pe_prep, 1)
            pe.wait_ge(prep, prep_at["wsi_n"])
            pe.matmul(bank_c[:, 0:PROJ], bs_row[:], wsi_n[:], start=True, stop=True).then_inc(pe_prep, 1)
            pe.wait_ge(s_dense, 16)
            pe.wait_ge(prep, prep_at["wd_centred"])
            for j in range(4):
                for n in range(4):
                    first = (4 * j + n) * TILE
                    for i in range(2):
                        mm = pe.matmul(bank_z[:, j, n * E:(n + 1) * E], dense_t[:, i, first:first + TILE], wd_t[:, i, :],
                                       start=(i == 0), stop=(i == 1))
                mm.then_inc(pe_prep, 1)
            for j in range(4):
                pe.wait_ge(prep, prep_at[f"x_row{j}"])
                if j < 2:
                    pe.wait_ge(prep, prep_at["ws_e"])
                else:
                    pe.wait_ge(prep, prep_at[f"x{j - 2}"])
                for n in range(4):
                    mm = pe.transpose(bank_m[j % 2][:, n * TILE:(n + 1) * TILE], x_row[:, n, :], ident[:])
                mm.then_inc(pe_prep, 1)
            for j in range(4):
                pe.wait_ge(prep, prep_at[f"x{j}"])
                pe.matmul(bank_z[:, j, :], ones[:], x_t[:, j * BANK:(j + 1) * BANK], start=True, stop=True)\
                    .then_inc(pe_prep, 1)
            pe.wait_ge(prep, prep_at["end"])
            pe.wait_ge(act_prep, 8)

            def prepare_rest():
                pe.wait_ge(prep, prep_at["fold_w"])
                pe.wait_ge(mix_lo, 8)
                for t in range(STEPS):
                    mm = pe.matmul(bank_d[0:65, :], fold_w[:, t, :], wl[:, t, :], start=(t == 0), stop=(t == STEPS - 1))
                mm.then_inc(pe_prep, 1)
                pe.wait_ge(s_top, 16 * 3)
                for k in range(4):
                    for c in range(3):
                        mm = pe.matmul(bank_a[:, k:k + 1], w1[:, c, k * P:(k + 1) * P], col["bl"][:, c:c + 1],
                                       start=(c == 0), stop=(c == 2))
                mm.then_inc(pe_prep, 1)

            def tile_work(t, par, more, load, inter, top):
                def turn(t, par, g):
                    if g == 0:
                        pe.wait_ge(gathered[par], (t - par + 2) * (16 * CHUNKS))
                    if g >= 2:
                        pe.wait_ge(turned_kept, 4 * t + g - 1)
                    for n, c in enumerate(GROUPS[g]):
                        mm = pe.transpose(bank_t[g % 2][:, n * P:(n + 1) * P], rows[par][:, c, :], ident[:])
                    mm.then_inc(turned, 1)

                def gram_product(t, g):
                    pe.wait_ge(turned_kept, 4 * t + g + 1)
                    if g == 0 and not (isinstance(t, int) and t == 0):
                        pe.wait_ge(y_kept, 8 * t)
                    if g >= 2:
                        pe.wait_ge(quad_done, 4 * t + g - 1)
                    for n, c in enumerate(GROUPS[g]):
                        mm = pe.matmul(bank_g[g % 2][:, n * P:(n + 1) * P], rows_t[:, c, :], gram[:],
                                       start=True, stop=True)
                    mm.then_inc(gram_done, 1)

                def z_banks_free(batches):
                    pe.wait_ge(z_kept_act, 3 * (t - 1) + batches)
                    if any(ZDVE[:batches]):
                        pe.wait_ge(z_kept_dve, ZDVE_TILE * (t - 1) + sum(n > 0 for n in ZDVE[:batches]))

                def interact(batch):
                    if batch == 0:
                        pe.wait_ge(x_placed, t)
                        if load:
                            pe.wait_ge(turned_kept, 4 * (t + 1))
                        if top:
                            pe.wait_ge(z_kept, t - 1)
                            if not (isinstance(t, int) and t == 2):
                                pe.wait_ge(out_kept, t - 2)
                    else:
                        z_banks_free(batch)
                    pe.wait_ge(r_ready, 4 * (t - 1) + -(-sum(ZBATCH[:batch + 1]) * ZBANKS * QUAD // (2 * SPB)))
                    per_bank = ZBATCH[batch]
                    first = sum(ZBATCH[:batch]) * ZBANKS
                    for n in range(per_bank * ZBANKS):
                        mm = pe.matmul(bank_z[:, n // per_bank, (n % per_bank) * ZCOLS:(n % per_bank + 1) * ZCOLS],
                                       r_vec[:, first + n, OTHERS:ZCOLS], r_vec[:, first + n, :], start=True, stop=True)
                    mm.then_inc(z_done, 1)

                def linear(steps):
                    if steps[0] == 0:
                        z_banks_free(3)
                        pe.wait_ge(sumx_placed, t)
                        pe.wait_ge(prep, prep_at["rest"])
                    for s in steps:
                        mm = pe.matmul(bank_l, zd[:, s, :], wl[:, s, :], start=(s == 0), stop=(s == STEPS - 1))
                    if steps[-1] == STEPS - 1:
                        mm.then_inc(l_done, 1)

                def turn_z():
                    pe.wait_ge(z_scaled, t)
                    for c in range(3):
                        mm = pe.transpose(bank_l[:, c * P:(c + 1) * P], z_row[:, c * P:(c + 1) * P], ident[:])
                    mm.then_inc(z_turned, 1)

                def mix(j):
                    pe.wait_ge(rows_scaled, 4 * t + j + 1)
                    if j < 2 and inter:
                        pe.wait_ge(mix_lo, 8 * t)
                    if j == 1 and top:
                        pe.wait_ge(h1_kept, t - 1)
                    if j >= 2:
                        pe.wait_ge(mix_lo, 8 * t + 2 * (j - 1))
                    wins = [w for w in WINDOWS if w[3] == j]
                    for n, (c, s0, k, _, w0) in enumerate(wins):
                        o = (s0 - j * SPB) * PROJ
                        mm = pe.matmul(bank_m[j % 2][:, o:o + k * PROJ], scaled[:, c, :], wsi_b[:, w0:w0 + k, :],
                                       start=(n == 0), stop=(n == len(wins) - 1), skip_group_check=True)
                    mm.then_inc(mix_done, 1)

                def project(j):
                    for blk in range(2):
                        pe.wait_ge(mix_lo, 8 * t + 2 * j + blk + 1)
                        if j == 0:
                            pe.wait_ge(quad_done, 4 * (t + 1))
                        else:
                            pe.wait_ge(y_kept, 8 * t + 2 * (j - 1) + blk + 1)
                        pe.matmul(bank_g[blk][:], proj_hi[:], mixed[:, j % 2, blk, :], start=True, stop=False)
                        pe.matmul(bank_g[blk][:], proj_lo[:], mixed[:, j % 2, blk, :], start=False, stop=True)\
                            .then_inc(y_done, 1)

                def first_layer(part):
                    if part == 0:
                        pe.wait_ge(z_kept, t - 1)
                        if load:
                            pe.wait_ge(mix_lo, 8 * t)
                        else:
                            pe.wait_ge(h1_kept, t - 2)
                    dense = [dense_t[:, i, bass.ds((t - 2) * TILE, TILE)] for i in range(2)]
                    for k in (2 * part, 2 * part + 1):
                        for c in range(5):
                            mm = pe.matmul(bank_d[:, k * TILE:(k + 1) * TILE], w1[:, c, k * P:(k + 1) * P],
                                           z_t[:, c, :] if c < 3 else dense[c - 3], start=(c == 0), stop=(c == 4))
                    if part == 1:
                        mm.then_inc(h1_done, 1)

                def second_layer():
                    pe.wait_ge(h1_kept, t - 1)
                    if inter:
                        z_banks_free(3)
                    for k in range(2):
                        for c in range(4):
                            mm = pe.matmul(bank_w[:, k * TILE:(k + 1) * TILE], w2[:, c, k * P:(k + 1) * P], h1[:, c, :],
                                           start=(c == 0), stop=(c == 3))
                    mm.then_inc(h2_done, 1)

                def third_layer():
                    pe.wait_ge(h2_kept, t - 1)
                    for c in range(2):
                        mm = pe.matmul(bank_w[0:1, 0:TILE], w3[:, c:c + 1], h2[:, c, :], start=(c == 0), stop=(c == 1))
                    mm.then_inc(out_done, 1)

                if load:
                    if not inter:
                        for g in range(len(GROUPS)):
                            turn(t, par, g)
                        gram_product(t, 0)
                        gram_product(t, 1)
                    gram_product(t, 2)
                    gram_product(t, 3)
                if top:
                    first_layer(0)
                if inter:
                    interact(0)
                if load:
                    mix(0)
                if top:
                    first_layer(1)
                if load:
                    project(0)
                if inter:
                    interact(1)
                if load:
                    mix(1)
                    mix(2)
                if inter:
                    interact(2)
                if load:
                    project(1)
                    mix(3)
                if inter:
                    linear(range(0, 3))
                if load:
                    project(2)
                if inter:
                    linear(range(3, 6))
                    linear(range(6, STEPS))
                if more:
                    turn(t + 1, 1 - par, 0)
                    turn(t + 1, 1 - par, 1)
                if load:
                    project(3)
                if top:
                    second_layer()
                if more:
                    turn(t + 1, 1 - par, 2)
                    gram_product(t + 1, 0)
                    gram_product(t + 1, 1)
                if top:
                    third_layer()
                if more:
                    turn(t + 1, 1 - par, 3)
                if inter:
                    turn_z()

            over_tiles(pe, tile_work, prepare_rest)

        @block.scalar
        def _(act):
            act.wait_ge(prep, prep_at["constants"])
            for j in range(4):
                act.wait_ge(pe_prep, 4 + j)
                for n in range(4):
                    t = 4 * j + n
                    ins = nc.scalar.activation(y_sq[:, j // 2, j % 2, n * E:(n + 1) * E], bank_z[:, j, n * E:(n + 1) * E],
                                               ACT.Square, accum_out=x_var[:, t:t + 1])
                ins.then_inc(x_squared, 1)
                act.wait_ge(x_squared, j + 1)
                nc.scalar.activation(x_std[:, 4 * j:4 * j + 4], x_var[:, 4 * j:4 * j + 4], ACT.Sqrt, bias=eps[:],
                                     scale=1.0 / E).then_inc(act_prep, 1)
            for j in range(4):
                act.wait_ge(pe_prep, 12 + j)
                nc.scalar.copy(sum_x[PROJ:PROJ + 1, j * BANK:(j + 1) * BANK], bank_z[PROJ:PROJ + 1, j, :])\
                    .then_inc(act_prep, 1)
            act.wait_ge(prep, prep_at["end"])

            def tile_work(t, par, more, load, inter, top):
                def keep_z(batch):
                    act.wait_ge(z_done, 3 * (t - 1) + batch + 1)
                    if batch == 0 and top:
                        act.wait_ge(l_done, t - 1)
                    for to, src in z_moves(batch)[0]:
                        ins = nc.scalar.copy(to, src)
                    ins.then_inc(z_kept_act, 1)

                def square(j):
                    for blk in range(2):
                        act.wait_ge(y_kept, 8 * t + 2 * j + blk + 1)
                        if blk == 0 and (inter or j >= 2):
                            act.wait_ge(y_var_done, 4 * t + j - 1)
                        nc.scalar.activation(y_sq[:, j % 2, blk, :], y[:, Y_PART[j], blk, :], ACT.Square)\
                            .then_inc(y_squared, 1)

                def y_root(t, j, inter):
                    act.wait_ge(y_var_done, 4 * t + j + 1)
                    if inter:
                        act.wait_ge(y_r_done, 4 * (t - 1) + j + 1)
                    nc.scalar.activation(y_std[:, j, :], y_var[:, j, :], ACT.Sqrt, bias=eps[:], scale=1.0 / PROJ)\
                        .then_inc(y_std_done, 1)

                def keep_high(j):
                    act.wait_ge(mix_done, 4 * t + j + 1)
                    for blk in range(2):
                        if inter or j >= 2:
                            act.wait_ge(y_done, 8 * t + 2 * j + blk - 3)
                        own = slice(D * blk, D * (blk + 1))
                        nc.scalar.copy(mixed[own, j % 2, blk, :], bank_m[j % 2][own, :]).then_inc(mix_hi, 1)

                def relu_1():
                    act.wait_ge(h1_done, t - 1)
                    if not (isinstance(t, int) and t == 2):
                        act.wait_ge(h2_done, t - 2)
                    for k in range(4):
                        ins = nc.scalar.activation(h1[:, k, :], bank_d[:, k * TILE:(k + 1) * TILE], ACT.Relu,
                                                   bias=b1[:, k:k + 1])
                    ins.then_inc(h1_kept, 1)

                def relu_2():
                    act.wait_ge(h2_done, t - 1)
                    if not (isinstance(t, int) and t == 2):
                        act.wait_ge(out_done, t - 2)
                    for k in range(2):
                        ins = nc.scalar.activation(h2[:, k, :], bank_w[:, k * TILE:(k + 1) * TILE], ACT.Relu,
                                                   bias=col["b2"][:, k:k + 1])
                    ins.then_inc(h2_kept, 1)

                def keep_out():
                    act.wait_ge(out_done, t - 1)
                    nc.scalar.copy(out_row[:, bass.ds((t - 2) * TILE, TILE)], bank_w[0:1, 0:TILE]).then_inc(out_kept, 1)

                def keep_turned(t, g):
                    act.wait_ge(turned, 4 * t + g + 1)
                    if not (isinstance(t, int) and t == 0):
                        act.wait_ge(gram_done, 4 * (t - 1) + g + 1)
                    cs = GROUPS[g]
                    nc.scalar.copy(rows_t[:, cs[0]:cs[-1] + 1, :],
                                   bank_t[g % 2][:, 0:len(cs) * P].rearrange("p (c n) -> p c n", n=P))\
                        .then_inc(turned_kept, 1)

                def row_root():
                    act.wait_ge(var_done, t + 1)
                    if inter:
                        act.wait_ge(rstd_done, t)
                    nc.scalar.activation(row_std[:], row_var[:], ACT.Sqrt, bias=eps[:]).then_inc(row_std_done, 1)

                def place_sum_x():
                    if top:
                        act.wait_ge(l_done, t - 1)
                    nc.scalar.copy(zd[PROJ:PROJ + 1, STEPS - 1, :],
                                   sum_x[PROJ:PROJ + 1, bass.ds((t - 1) * TILE, TILE)]).then_inc(sumx_placed, 1)

                def place_x():
                    if inter:
                        act.wait_ge(z_done, 3 * t)
                    nc.scalar.copy(r_vec[:, :, 0:QUAD], x_t[:, bass.ds(t * TILE, TILE)].rearrange("p (g j) -> p g j", j=QUAD))\
                        .then_inc(x_placed, 1)

                def linear_root():
                    act.wait_ge(l_done, t)
                    nc.scalar.activation(l_sq[:], bank_l, ACT.Square, accum_out=l_var[:]).then_inc(l_var_done, 1)
                    act.wait_ge(l_var_done, t)
                    if top:
                        act.wait_ge(l_r_done, t - 1)
                    nc.scalar.activation(l_std[:], l_var[:], ACT.Sqrt, bias=eps[:], scale=1.0 / MAXD)\
                        .then_inc(l_std_done, 1)

                def scale_z():
                    act.wait_ge(l_r_done, t)
                    if top:
                        act.wait_ge(z_turned, t - 1)
                    nc.scalar.activation(z_row[:], bank_l[:, 0:USED], ACT.Copy, scale=l_r[:]).then_inc(z_scaled, 1)

                def keep_turned_z():
                    act.wait_ge(z_turned, t)
                    if top:
                        act.wait_ge(h1_done, t - 1)
                    nc.scalar.copy(z_t[:], bank_l[:, 0:USED].rearrange("p (c b) -> p c b", c=3)).then_inc(z_kept, 1)

                if load:
                    if not inter:
                        for g in range(len(GROUPS)):
                            keep_turned(t, g)
                if inter:
                    y_root(t - 1, 3, top)
                if load:
                    row_root()
                    keep_high(0)
                if inter:
                    keep_z(0)
                if top:
                    relu_1()
                if load:
                    square(0)
                if inter:
                    keep_z(1)
                if load:
                    keep_high(1)
                    keep_high(2)
                if inter:
                    place_sum_x()
                if load:
                    y_root(t, 0, inter)
                if inter:
                    keep_z(2)
                if load:
                    square(1)
                    place_x()
                    keep_high(3)
                    y_root(t, 1, inter)
                    square(2)
                if more:
                    keep_turned(t + 1, 0)
                if load:
                    y_root(t, 2, inter)
                if more:
                    keep_turned(t + 1, 1)
                if inter:
                    linear_root()
                if top:
                    relu_2()
                if load:
                    square(3)
                if more:
                    keep_turned(t + 1, 2)
                if top:
                    keep_out()
                if inter:
                    scale_z()
                if more:
                    keep_turned(t + 1, 3)
                if inter:
                    keep_turned_z()

            over_tiles(act, tile_work)


def column(a, n=1):
    return np.asarray(a).reshape(n, P).T


def laid_out(x):
    f32 = np.float32
    tables = [np.asarray(x[f"tbl_{f}"]) for f in range(N_SP)]
    first_row = np.cumsum([0] + [t.shape[0] for t in tables])[:-1]
    feature = (np.arange(CHUNKS * P) % N_SP).reshape(CHUNKS, P)
    ids = np.asarray(x["ids"]).reshape(TILES, MIX_BANKS, 2, SPB, N_SP).transpose(0, 2, 1, 3, 4)
    ids = ids.reshape(TILES, 2, CHUNKS, P).transpose(3, 0, 2, 1)
    wsi = np.asarray(x["L0_rec_Wsi"])
    wsi_b = np.zeros((P, WIN_COLS, PROJ), f32)
    for c, s0, k, bank, w0 in WINDOWS:
        for r in range(P):
            s, n = divmod(c * P + r, N_SP)
            if s0 <= s < s0 + k and s // SPB == bank:
                wsi_b[r, w0 + s - s0] = wsi[:, n]
    lin = np.asarray(x["L0_rec_Wl"])
    gsi, bsi = np.asarray(x["L0_rec_gsi"]), np.asarray(x["L0_rec_bsi"])
    wl = np.zeros((P, STEPS, MAXD), f32)
    gsi_q = np.ones((P, STEPS), f32)
    bsi_q = np.zeros((P, STEPS), f32)
    mask_a = np.zeros((P, 64), f32)
    mask_b = np.zeros((P, STEPS, 64), f32)
    for k in range(4):
        quarter = slice(PROJ * k, PROJ * (k + 1))
        mask_a[quarter, 0:PROJ] = np.eye(PROJ, dtype=f32)
        for t in range(QPK):
            q = QPK * k + t
            gsi_q[quarter, t] = gsi[q]
            bsi_q[quarter, t] = bsi[q]
            mask_b[quarter, t, q] = 1.0
            for p in range(q + 1, PROJ):
                wl[PROJ * k + p, t] = lin[:, (p + 1) * p // 2 + q + 1]
    for p in range(PROJ):
        wl[p, QPK] = lin[:, (p + 1) * p // 2]
    mask_b[0:PROJ, QPK, PROJ] = 1.0
    cols = {
        "gd": column(x["L0_rec_gd"]), "bd": column(x["L0_rec_bd"]),
        "gsi_p": np.tile(gsi, 4)[:, None], "bsi_p": np.tile(bsi, 4)[:, None],
        "gsi_q": gsi_q, "bsi_q": bsi_q,
        "gl": column(np.asarray(x["L0_rec_gl"])[:USED], 3), "bl": column(np.asarray(x["L0_rec_bl"])[:USED], 3),
        "b1": column(x["b_top1"], 4), "b2": column(x["b_top2"], 2),
    }
    top1 = np.asarray(x["W_top1"])
    top1 = np.concatenate([top1[:USED], top1[MAXD:]])
    dense_t = np.asarray(x["r_dense_t"]).T
    ws = np.asarray(x["L0_rec_Ws"])
    arrays = {
        "table": np.concatenate(tables),
        "ids": ids.reshape(P, -1),
        "row_base": np.repeat(first_row[feature].T, 2, axis=1).astype(np.int32),
        "ident": np.eye(P, dtype=f32),
        "ws_t": np.concatenate([ws.T, ws.T]),
        "gs_row": np.broadcast_to(np.asarray(x["L0_rec_gs"]), (P, E)),
        "bs_row": np.broadcast_to(np.asarray(x["L0_rec_bs"]), (N_SP, E)),
        "wsi_n": wsi.T, "wsi_b": wsi_b, "wl": wl, "mask_a": mask_a, "mask_b": mask_b,
        "wd_t": np.asarray(x["L0_rec_Wd"]).T.reshape(2, P, E).transpose(1, 0, 2),
        "dense_t": dense_t.reshape(2, P, B).transpose(1, 0, 2),
        "cols": np.concatenate([cols[name] for name, _ in COLS], axis=1),
        "w1": top1.reshape(5, P, H1).transpose(1, 0, 2),
        "w2": np.asarray(x["W_top2"]).reshape(4, P, H2).transpose(1, 0, 2),
        "w3": column(x["W_top3"], 2),
    }
    return {name: np.ascontiguousarray(a) for name, a in arrays.items()}


def kernel(**inputs):
    import concourse.bacc as bacc
    from concourse.bass_utils import run_bass_kernel_spmd

    nc = bacc.Bacc("TRN2", target_bir_lowering=False, num_devices=1)
    arrays = laid_out(inputs)
    io = {name: nc.dram_tensor(f"in_{name}", a.shape, mybir.dt.from_np(a.dtype), kind="ExternalInput").ap()
          for name, a in arrays.items()}
    io["out"] = nc.dram_tensor("out", (B, 1), F32, kind="ExternalOutput").ap()
    tower(nc, io)
    r = run_bass_kernel_spmd(nc, [{f"in_{name}": a for name, a in arrays.items()}], core_ids=[0])
    return r.results[0]["out"]
```

```python
from contextlib import ExitStack

import numpy as np

import concourse.bass as bass
from concourse import mybir

F32 = mybir.dt.float32
F32R = mybir.dt.float32r
I32 = mybir.dt.int32
ALU = mybir.AluOpType
ACT = mybir.ActivationFunctionType
AX_X = mybir.AxisListType.X

P = 128
B = 2048
N_SP, D = 26, 64
D_DENSE = 256
E = 128
PROJ = 32
MAXD, USED = 512, 384
H1, H2 = 512, 256
EPS = 1e-5

TILE = 128
TILES = B // TILE
BLK = TILE // 2
CHUNKS = BLK * N_SP // P
GROUPS = [range(c, min(c + 4, CHUNKS)) for c in range(0, CHUNKS, 4)]
BANK = 512
SPB = BANK // PROJ
MIX_BANKS = BLK // SPB

QUAD = 4
OTHERS = QUAD + 1
ZCOLS = OTHERS + QUAD * PROJ
QUADS = TILE // QUAD
QPK = PROJ // 4
STEPS = QPK + 1
Y_PART = [0, 1, 2, 0]
ZBANKS = 4
ZBATCH = [3, 3, 2]
ZDVE = [1, 2, 1]
ZDVE_TILE = sum(n > 0 for n in ZDVE)


COLS = [("gd", 1), ("bd", 1), ("gsi_p", 1), ("bsi_p", 1), ("gsi_q", STEPS), ("bsi_q", STEPS), ("gl", 3), ("bl", 3),
        ("b1", 4), ("b2", 2)]


def chunk_windows():
    out, at = [], 0
    for c in range(CHUNKS):
        first, last = c * P // N_SP, (c * P + P - 1) // N_SP
        while first <= last:
            bank = first // SPB
            end = min(last + 1, (bank + 1) * SPB)
            n = max(end - first, 3)
            start = min(first, (bank + 1) * SPB - n)
            out.append((c, start, n, bank, at))
            at += n
            first = end
    return out, at


def last_batch(j):
    return min(b for b in range(3) if sum(ZBATCH[:b + 1]) * ZBANKS * QUAD >= (j + 1) * 2 * SPB)


WINDOWS, WIN_COLS = chunk_windows()


def tower(nc, io):
    with ExitStack() as ctx:
        def sb(name, shape, dt=F32):
            return ctx.enter_context(nc.sbuf_tensor(name, shape, dt))

        def sem(name):
            return ctx.enter_context(nc.semaphore(name))

        bank_a, bank_b, bank_c, bank_d = (
            ctx.enter_context(nc.psum_tensor(f"bank_{n}", [P, BANK], F32)) for n in "abcd")
        bank_z = ctx.enter_context(nc.psum_tensor("bank_z", [P, ZBANKS, BANK], F32))

        ident = sb("ident", [P, P])
        ones = sb("ones", [P, P])
        eps = sb("eps", [P, 1])
        ids_all = sb("ids_all", [P, TILES * 2 * CHUNKS], I32)
        row_base = sb("row_base", [P, 2 * CHUNKS], I32)
        ws_t = sb("ws_t", [P, E])
        gs_row = sb("gs_row", [P, E])
        ws_e = sb("ws_e", [P, P])
        gram = sb("gram", [P, P])
        proj_hi = sb("proj_hi", [P, E], F32R)
        proj_lo = sb("proj_lo", [P, E], F32R)
        wd_t = sb("wd_t", [P, 2, E])
        wsi_b = sb("wsi_b", [P, WIN_COLS, PROJ])
        wsi_n = sb("wsi_n", [N_SP, PROJ])
        bs_row = sb("bs_row", [N_SP, E])
        y_bias = sb("y_bias", [P, PROJ])
        wl = sb("wl", [P, STEPS, MAXD])
        fold_w = sb("fold_w", [P, STEPS, 65])
        mask_a = sb("mask_a", [P, 64])
        mask_b = sb("mask_b", [P, STEPS, 64])
        cols = sb("cols", [P, sum(n for _, n in COLS)])
        w1 = sb("w1", [P, 5, H1])
        w2 = sb("w2", [P, 4, H2])
        w3 = sb("w3", [P, 2])
        means = sb("means", [P, 160])
        b1 = sb("b1", [P, 4])
        col = {}
        at = 0
        for name, n in COLS:
            col[name] = cols[:, at:at + n]
            at += n

        dense_t = sb("dense_t", [P, 2, B])
        x_t = sb("x_t", [P, B])
        sum_x = sb("sum_x", [P, B])

        ids = [sb(f"ids{i}", [P, 2 * CHUNKS], I32) for i in range(2)]
        rows = [sb(f"rows{i}", [P, CHUNKS, 2 * D]) for i in range(2)]
        rows_t = sb("rows_t", [P, CHUNKS, P])
        scaled = sb("scaled", [P, CHUNKS, 2 * D])
        row_var = sb("row_var", [P, 2 * CHUNKS])
        row_std = sb("row_std", [P, 2 * CHUNKS])
        row_r = sb("row_r", [P, 2 * CHUNKS])
        mixed = sb("mixed", [P, 2, 2, BANK], F32R)
        y = sb("y", [P, 3, 2, BANK])
        y_sq = sb("y_sq", [P, 2, 2, BANK])
        y_var = sb("y_var", [P, MIX_BANKS, 2 * SPB])
        y_std = sb("y_std", [P, MIX_BANKS, 2 * SPB])
        y_r = sb("y_r", [P, MIX_BANKS, 2 * SPB])
        r_vec = sb("r_vec", [P, QUADS, ZCOLS])
        zd = sb("zd", [P, STEPS, TILE])
        l_sq = sb("l_sq", [P, MAXD])
        l_var = sb("l_var", [P, 1])
        l_std = sb("l_std", [P, 1])
        l_r = sb("l_r", [P, 1])
        z_row = sb("z_row", [P, USED])
        z_t = sb("z_t", [P, 3, TILE])
        h1 = sb("h1", [P, 4, TILE])
        h2 = sb("h2", [P, 2, TILE])
        x_row = [sb(f"x_row{i}", [P, 4, E]) for i in range(2)]
        x_var = sb("x_var", [P, TILES])
        x_std = sb("x_std", [P, TILES])
        x_r = sb("x_r", [P, TILES])
        out_row = sb("out_row", [1, B])

        s_ids, s_small, s_wsi, s_wl, s_dense, s_top = (
            sem(n) for n in ("ids_loaded", "small_loaded", "wsi_loaded", "wl_loaded", "dense_loaded", "top_loaded"))
        gathered = [[sem(f"gathered_{parity}_{g}") for g in range(len(GROUPS))] for parity in ("even", "odd")]
        ids_ready = sem("ids_ready")
        ids_seen = sem("ids_seen")
        prep = sem("prep")
        pe_prep = sem("pe_prep")
        act_prep = sem("act_prep")
        fold_done = sem("fold_done")
        wl_scaled = sem("wl_scaled")
        wl_centred = sem("wl_centred")
        bl_done = sem("bl_done")
        sum_x_done = sem("sum_x_done")
        sum_x_kept = sem("sum_x_kept")
        x_squared = sem("x_squared")
        turned = sem("turned")
        turned_kept = sem("turned_kept")
        gram_done = sem("gram_done")
        quad_done = sem("quad_done")
        var_done = sem("var_done")
        rstd_done = sem("rstd_done")
        rows_scaled = sem("rows_scaled")
        row_std_done = sem("row_std_done")
        mix_done = sem("mix_done")
        mix_hi = sem("mix_hi")
        mix_lo = sem("mix_lo")
        y_done = sem("y_done")
        y_kept = sem("y_kept")
        y_squared = sem("y_squared")
        y_var_done = sem("y_var_done")
        y_std_done = sem("y_std_done")
        y_r_done = sem("y_r_done")
        r_ready = sem("r_ready")
        x_placed = sem("x_placed")
        z_done = sem("z_done")
        z_kept_act = sem("z_kept_act")
        z_kept_dve = sem("z_kept_dve")
        sumx_placed = sem("sumx_placed")
        l_done = sem("l_done")
        l_var_done = sem("l_var_done")
        l_std_done = sem("l_std_done")
        l_r_done = sem("l_r_done")
        z_scaled = sem("z_scaled")
        z_turned = sem("z_turned")
        z_kept = sem("z_kept")
        h1_done, h1_kept, h2_done, h2_kept, out_done, out_kept = (
            sem(n) for n in ("h1_done", "h1_kept", "h2_done", "h2_kept", "out_done", "out_kept"))
        stored = sem("stored")

        bank_g = [bank_b, bank_c]
        bank_m = [bank_a, bank_d]
        bank_l = bank_z[:, 3, :]
        bank_w = bank_z[:, 2, :]
        bank_t = [bank_z[:, i, :] for i in range(2)]

        def z_moves(batch):
            per_bank = ZBATCH[batch]
            first = sum(ZBATCH[:batch]) * ZBANKS * QUAD
            n = per_bank * ZBANKS * QUAD
            out = []
            for j in range(QUAD):
                src = bank_z[PROJ * j:PROJ * (j + 1), :, 0:per_bank * ZCOLS]
                src = src.rearrange("p n (g c) -> p n g c", c=ZCOLS)

                def to(k, t0, t1, j=j):
                    v = zd[PROJ * k:PROJ * (k + 1), t0:t1, first:first + n]
                    return v.rearrange("p t (n g j) -> p n g j t", n=ZBANKS, j=QUAD)[:, :, :, j, :]

                for k in range(4):
                    c = OTHERS + PROJ * j + QPK * k
                    out.append((to(k, 0, QPK), src[:, :, :, c:c + QPK]))
                out.append((to(0, QPK, STEPS), src[:, :, :, j:j + 1]))
                out.append((to(3, QPK, STEPS), src[:, :, :, QUAD:QUAD + 1]))
            cut = 6 * (QUAD - ZDVE[batch])
            return out[:cut], out[cut:]

        prep_at = {}

        block = ctx.enter_context(nc.Block())

        def over_tiles(eng, body):
            body(0, 0, True, True, False, False)
            body(1, 1, True, True, True, False)
            body(2, 0, True, True, True, True)
            body(3, 1, True, True, True, True)
            with eng.Fori(2, TILES // 2 - 1) as i:
                body(i * 2, 0, True, True, True, True)
                body(i * 2 + 1, 1, True, True, True, True)
            body(TILES - 2, 0, True, True, True, True)
            body(TILES - 1, 1, False, True, True, True)
            body(TILES, 0, False, False, True, True)
            body(TILES + 1, 1, False, False, False, True)

        @block.vector
        def _(dve):
            count = [0]

            def step(ins, name=None):
                count[0] += 1
                ins.then_inc(prep, 1)
                if name:
                    assert name not in prep_at
                    prep_at[name] = count[0]
                dve.wait_ge(prep, count[0])

            v = nc.vector
            step(v.memset(eps[:], EPS))
            step(v.memset(ones[:], 1.0), "constants")
            dve.wait_ge(s_small, 16 * 7)
            step(v.tensor_reduce(means[:, 0:1], ws_t[:], AX_X, ALU.add))
            step(v.tensor_scalar(means[:, 0:1], means[:, 0:1], -1.0 / E, None, ALU.mult))
            step(v.tensor_scalar(ws_t[:], ws_t[:], means[:, 0:1], None, ALU.add), "ws_centred")
            step(v.memset(gram[:], 0.0))
            step(v.tensor_tensor(gs_row[:], ws_t[:], gs_row[:], ALU.mult))
            step(v.tensor_copy(proj_hi[:], gs_row[:]))
            step(v.tensor_tensor(proj_lo[:], gs_row[:], proj_hi[:].bitcast(F32), ALU.subtract))
            dve.wait_ge(pe_prep, 1)
            step(v.tensor_copy(ws_e[:], bank_a[:, 0:P]), "ws_e")
            step(v.tensor_reduce(means[0:N_SP, 0:1], wsi_n[:], AX_X, ALU.add))
            step(v.tensor_scalar(means[0:N_SP, 0:1], means[0:N_SP, 0:1], -1.0 / PROJ, None, ALU.mult))
            step(v.tensor_scalar(wsi_n[:], wsi_n[:], means[0:N_SP, 0:1], None, ALU.add), "wsi_n")
            step(v.tensor_reduce(means[:, 0:2], wd_t[:], AX_X, ALU.add))
            step(v.tensor_scalar(means[:, 0:2], means[:, 0:2], -1.0 / E, None, ALU.mult))
            for i in range(2):
                step(v.tensor_scalar(wd_t[:, i, :], wd_t[:, i, :], means[:, i:i + 1], None, ALU.add),
                     "wd_centred" if i else None)
            dve.wait_ge(pe_prep, 2)
            for blk in range(2):
                half = slice(blk * D, (blk + 1) * D)
                step(v.tensor_scalar(gram[half, half], bank_b[half, half], 1.0 / E, None, ALU.mult),
                     "gram" if blk else None)
            dve.wait_ge(pe_prep, 3)
            step(v.tensor_copy(y_bias[:], bank_c[:, 0:PROJ]), "y_bias")
            dve.wait_ge(s_wsi, 16)
            m = means[:, 0:WIN_COLS]
            step(v.tensor_reduce(m, wsi_b[:], AX_X, ALU.add))
            step(v.tensor_scalar(m, m, -1.0 / PROJ, None, ALU.mult))
            step(v.tensor_tensor(wsi_b[:], wsi_b[:],
                                 m.rearrange("p (w o) -> p w o", o=1).broadcast_to([P, WIN_COLS, PROJ]), ALU.add))
            step(v.memset(r_vec[:, :, QUAD:OTHERS], 1.0))
            step(v.memset(zd[:, STEPS - 1, :], 0.0))
            step(v.memset(zd[64:65, STEPS - 1, :], 1.0))

            def scale_x(j):
                four = slice(4 * j, 4 * j + 4)
                dve.wait_ge(act_prep, j + 1)
                step(v.reciprocal(x_r[:, four], x_std[:, four]))
                if j >= 2:
                    dve.wait_ge(pe_prep, 8 + j - 2)
                step(v.tensor_tensor(x_row[j % 2][:], bank_z[:, j, :].rearrange("b (t e) -> b t e", t=4),
                                     x_r[:, four].rearrange("b (t o) -> b t o", o=1).broadcast_to([P, 4, E]),
                                     ALU.mult), f"x_row{j}")

            def finish_x(j):
                dve.wait_ge(pe_prep, 8 + j)
                step(v.tensor_scalar(x_t[:, j * BANK:(j + 1) * BANK], bank_m[j % 2][:], col["gd"], col["bd"],
                                     ALU.mult, ALU.add), "end" if j == 3 else f"x{j}")

            scale_x(0)
            for j in range(3):
                scale_x(j + 1)
                finish_x(j)

            dve.wait_ge(s_wl, 16 * 3)
            bq = col["bsi_q"].rearrange("p (t o) -> p t o", o=1)
            fw = fold_w[:, :, 0:64]
            step(v.tensor_tensor(fw, mask_a[:].rearrange("p (o n) -> p o n", o=1).broadcast_to([P, STEPS, 64]),
                                 bq.broadcast_to([P, STEPS, 64]), ALU.mult))
            step(v.scalar_tensor_tensor(out=fw, in0=mask_b[:], scalar=col["bsi_p"], in1=fw, op0=ALU.mult, op1=ALU.add))
            step(v.tensor_scalar(fold_w[:, :, 64:65], bq, col["bsi_p"], float(E), ALU.mult, ALU.mult))
            step(v.tensor_scalar(col["gsi_q"], col["gsi_q"], col["gsi_p"], None, ALU.mult), "fold_w")
            finish_x(3)

            def last_step_weights():
                dve.wait_ge(fold_done, 1)
                last = wl[:, QPK, :]
                step(v.tensor_scalar(last, last, col["gsi_q"][:, QPK:STEPS], None, ALU.mult))
                step(v.tensor_scalar(wl[3 * PROJ:P, QPK, :], bank_l[0:PROJ, :], col["gsi_p"][0:PROJ, :], None, ALU.mult))
                step(v.tensor_copy(wl[32:33, QPK, :], bank_l[32:33, :]))
                step(v.tensor_copy(wl[64:65, QPK, :], bank_l[64:65, :]))
                step(v.tensor_reduce(means[:, QPK:STEPS], last, AX_X, ALU.add))

            def top_weights():
                dve.wait_ge(bl_done, 1)
                step(v.tensor_tensor(b1[:], bank_w[:, 0:4], col["b1"], ALU.add))
                for c in range(3):
                    step(v.tensor_scalar(w1[:, c, :], w1[:, c, :], col["gl"][:, c:c + 1], None, ALU.mult),
                         "w1" if c == 2 else None)

            def linear_means():
                dve.wait_ge(wl_scaled, QPK)
                step(v.tensor_scalar(means[:, 0:STEPS], means[:, 0:STEPS], -1.0 / MAXD, None, ALU.mult), "wl_means")

            def tile_work(t, par, more, load, inter, top):
                def keep_z(batch):
                    if not ZDVE[batch]:
                        return
                    dve.wait_ge(z_done, 3 * (t - 1) + batch + 1)
                    if batch == 0 and top:
                        dve.wait_ge(l_done, t - 1)
                    for to, src in z_moves(batch)[1]:
                        ins = v.tensor_copy(to, src)
                    ins.then_inc(z_kept_dve, 1)

                def keep_low(j):
                    for blk in range(2):
                        own, other = slice(D * blk, D * (blk + 1)), slice(D * (1 - blk), D * (2 - blk))
                        dve.wait_ge(mix_hi, 8 * t + 2 * j + blk + 1)
                        if inter or j >= 2:
                            dve.wait_ge(y_done, 8 * t + 2 * j + blk - 3)
                        v.tensor_tensor(mixed[other, j % 2, blk, :], bank_m[j % 2][own, :],
                                        mixed[own, j % 2, blk, :].bitcast(F32), ALU.subtract).then_inc(mix_lo, 1)

                def keep_y(j):
                    for blk in range(2):
                        dve.wait_ge(y_done, 8 * t + 2 * j + blk + 1)
                        if j == 3:
                            dve.wait_ge(y_squared, 8 * t + blk + 1)
                            dve.wait_ge(r_ready, 4 * t + 1)
                        elif inter:
                            dve.wait_ge(y_squared, 8 * t)
                            dve.wait_ge(r_ready, 4 * t)
                        v.tensor_tensor(
                            y[:, Y_PART[j], blk, :].rearrange("e (s p) -> e s p", p=PROJ),
                            bank_g[blk][:].rearrange("e (s p) -> e s p", p=PROJ),
                            y_bias[:].rearrange("e (o p) -> e o p", o=1).broadcast_to([P, SPB, PROJ]),
                            ALU.add).then_inc(y_kept, 1)

                def y_mean_square(j):
                    dve.wait_ge(y_squared, 8 * t + 2 * j + 2)
                    if inter:
                        dve.wait_ge(y_std_done, 4 * (t - 1) + j + 1)
                    v.tensor_reduce(y_var[:, j, :], y_sq[:, j % 2, :, :].rearrange("e a (s p) -> e (a s) p", p=PROJ),
                                    AX_X, ALU.add).then_inc(y_var_done, 1)

                def y_scale(t, j, inter):
                    dve.wait_ge(y_std_done, 4 * t + j + 1)
                    if inter:
                        dve.wait_ge(r_ready, 4 * (t - 1) + j + 1)
                    v.reciprocal(y_r[:, j, :], y_std[:, j, :]).then_inc(y_r_done, 1)
                    dve.wait_ge(y_r_done, 4 * t + j + 1)
                    if inter:
                        dve.wait_ge(z_done, 3 * (t - 1) + last_batch(j) + 1)
                    for blk in range(2):
                        quad = (2 * j + blk) * (SPB // QUAD)
                        ins = v.tensor_tensor(
                            r_vec[:, quad:quad + SPB // QUAD, OTHERS:ZCOLS].rearrange("e g (s p) -> e g s p", p=PROJ),
                            y[:, Y_PART[j], blk, :].rearrange("e (g s p) -> e g s p", g=SPB // QUAD, p=PROJ),
                            y_r[:, j, blk * SPB:(blk + 1) * SPB].rearrange("e (g s o) -> e g s o", s=QUAD, o=1)
                            .broadcast_to([P, SPB // QUAD, QUAD, PROJ]), ALU.mult)
                    ins.then_inc(r_ready, 1)

                def square_form(g):
                    dve.wait_ge(gram_done, 4 * t + g + 1)
                    if inter:
                        dve.wait_ge(mix_done, 4 * t)
                    a, b = GROUPS[g][0], GROUPS[g][-1] + 1
                    v.tensor_tensor(scaled[:, a:b, :],
                                    bank_g[g % 2][:, 0:(b - a) * P].rearrange("p (c n) -> p c n", n=P),
                                    rows[par][:, a:b, :], ALU.mult).then_inc(quad_done, 1)

                def row_mean_square():
                    dve.wait_ge(quad_done, 4 * (t + 1))
                    if inter:
                        dve.wait_ge(row_std_done, t)
                    v.tensor_reduce(row_var[:], scaled[:].rearrange("p c (a d) -> p (c a) d", d=D), AX_X, ALU.add)\
                        .then_inc(var_done, 1)

                def row_reciprocal():
                    dve.wait_ge(row_std_done, t + 1)
                    if inter:
                        dve.wait_ge(rows_scaled, 4 * t)
                    v.reciprocal(row_r[:], row_std[:]).then_inc(rstd_done, 1)

                def scale_rows(groups):
                    dve.wait_ge(rstd_done, t + 1)
                    dve.wait_ge(var_done, t + 1)
                    for g in groups:
                        a, b = GROUPS[g][0], GROUPS[g][-1] + 1
                        v.tensor_tensor(scaled[:, a:b, :].rearrange("p c (a d) -> p (c a) d", d=D),
                                        rows[par][:, a:b, :].rearrange("p c (a d) -> p (c a) d", d=D),
                                        row_r[:, 2 * a:2 * b].rearrange("p (n o) -> p n o", o=1)
                                        .broadcast_to([P, 2 * (b - a), D]), ALU.mult).then_inc(rows_scaled, 1)

                def linear_reciprocal():
                    dve.wait_ge(l_std_done, t)
                    if top:
                        dve.wait_ge(z_scaled, t - 1)
                    v.reciprocal(l_r[:], l_std[:]).then_inc(l_r_done, 1)

                if load:
                    square_form(0)
                    square_form(1)
                    square_form(2)
                    square_form(3)
                    row_mean_square()
                    row_reciprocal()
                    scale_rows([0])
                if inter:
                    keep_z(0)
                if load:
                    scale_rows([1])
                    scale_rows([2])
                    keep_low(0)
                if inter:
                    y_scale(t - 1, 3, top)
                if load:
                    scale_rows([3])
                    keep_y(0)
                if inter:
                    keep_z(1)
                if load:
                    y_mean_square(0)
                    keep_low(1)
                if inter:
                    keep_z(2)
                if load and not inter:
                    last_step_weights()
                if load:
                    keep_y(1)
                    keep_low(2)
                    keep_low(3)
                    keep_y(2)
                    y_mean_square(1)
                    y_scale(t, 0, inter)
                    y_mean_square(2)
                    keep_y(3)
                    y_scale(t, 1, inter)
                    y_mean_square(3)
                if inter:
                    linear_reciprocal()
                if load:
                    y_scale(t, 2, inter)
                if inter and not top:
                    top_weights()
                if load and not inter:
                    linear_means()

            over_tiles(dve, tile_work)

        @block.sync
        def _(sp):
            for dst, src in ((ids_all, "ids"), (row_base, "row_base")):
                sp.dma_start(dst[:], io[src]).then_inc(s_ids, 16)
            for dst, src in ((ws_t, "ws_t"), (gs_row, "gs_row"), (ident, "ident"), (cols, "cols"),
                             (wd_t, "wd_t"), (wsi_n, "wsi_n"), (bs_row, "bs_row")):
                sp.dma_start(dst[:], io[src]).then_inc(s_small, 16)
            sp.dma_start(dense_t[:], io["dense_t"]).then_inc(s_dense, 16)
            sp.dma_start(wsi_b[:], io["wsi_b"]).then_inc(s_wsi, 16)
            for dst, src in ((wl, "wl"), (mask_a, "mask_a"), (mask_b, "mask_b")):
                sp.dma_start(dst[:], io[src]).then_inc(s_wl, 16)
            for dst, src in ((w1, "w1"), (w2, "w2"), (w3, "w3")):
                sp.dma_start(dst[:], io[src]).then_inc(s_top, 16)
            sp.wait_ge(out_kept, TILES)
            sp.dma_start(io["out"].rearrange("b o -> o b"), out_row[:]).then_inc(stored, 16)
            sp.wait_ge(stored, 16)

        @block.gpsimd
        def _(pool):
            pool.wait_ge(s_ids, 32)

            def gather(t, par, more, load, inter, top):
                if not load:
                    return
                if top:
                    pool.wait_ge(rows_scaled, len(GROUPS) * (t - 1))
                if top:
                    for g in range(len(GROUPS)):
                        pool.wait_ge(gathered[par][g], (t - par) * (16 * len(GROUPS[g])))
                nc.gpsimd.tensor_tensor(ids[par][:], ids_all[:, bass.ds(t * (2 * CHUNKS), 2 * CHUNKS)],
                                        row_base[:], ALU.add).then_inc(ids_ready, 1)
                pool.wait_ge(ids_ready, t + 1)
                pool.sem_inc(ids_seen, 1)
                for n in range(2 * CHUNKS):
                    c, blk = divmod(n, 2)
                    nc.gpsimd.indirect_dma_start(
                        rows[par][:, c, D * blk:D * (blk + 1)], None, io["table"],
                        bass.IndirectOffsetOnAxis(ap=ids[par][:, n:n + 1], axis=0)).then_inc(gathered[par][c // len(GROUPS[0])], 16)

            over_tiles(pool, gather)

        @block.tensor
        def _(pe):
            pe.wait_ge(s_small, 16 * 7)
            pe.wait_ge(prep, prep_at["ws_centred"])
            pe.transpose(bank_a[:, 0:P], ws_t[:], ident[:]).then_inc(pe_prep, 1)
            pe.wait_ge(prep, prep_at["ws_e"])
            pe.matmul(bank_b[:, 0:P], ws_e[:], ws_e[:], start=True, stop=True).then_inc(pe_prep, 1)
            pe.wait_ge(prep, prep_at["wsi_n"])
            pe.matmul(bank_c[:, 0:PROJ], bs_row[:], wsi_n[:], start=True, stop=True).then_inc(pe_prep, 1)
            pe.wait_ge(s_dense, 16)
            pe.wait_ge(prep, prep_at["wd_centred"])
            for j in range(4):
                for n in range(4):
                    first = (4 * j + n) * TILE
                    for i in range(2):
                        mm = pe.matmul(bank_z[:, j, n * E:(n + 1) * E], dense_t[:, i, first:first + TILE], wd_t[:, i, :],
                                       start=(i == 0), stop=(i == 1))
                mm.then_inc(pe_prep, 1)
            for j in range(4):
                pe.wait_ge(prep, prep_at[f"x_row{j}"])
                if j < 2:
                    pe.wait_ge(prep, prep_at["ws_e"])
                else:
                    pe.wait_ge(prep, prep_at[f"x{j - 2}"])
                for n in range(4):
                    mm = pe.transpose(bank_m[j % 2][:, n * TILE:(n + 1) * TILE], x_row[j % 2][:, n, :], ident[:])
                mm.then_inc(pe_prep, 1)
            pe.wait_ge(prep, prep_at["end"])

            def fold(steps):
                for t in steps:
                    mm = pe.matmul(bank_l[0:65, :], fold_w[:, t, :], wl[:, t, :], start=(t == 0), stop=(t == STEPS - 1))
                if steps[-1] == STEPS - 1:
                    mm.then_inc(fold_done, 1)

            def add_up_x(j):
                if j:
                    pe.wait_ge(sum_x_kept, j)
                pe.matmul(bank_w, ones[:], x_t[:, j * BANK:(j + 1) * BANK], start=True, stop=True)\
                    .then_inc(sum_x_done, 1)

            def fold_bl():
                pe.wait_ge(s_top, 16 * 3)
                pe.wait_ge(sum_x_kept, 4)
                for k in range(4):
                    for c in range(3):
                        mm = pe.matmul(bank_w[:, k:k + 1], w1[:, c, k * P:(k + 1) * P], col["bl"][:, c:c + 1],
                                       start=(c == 0), stop=(c == 2))
                mm.then_inc(bl_done, 1)

            def tile_work(t, par, more, load, inter, top):
                def turn(t, par, g):
                    pe.wait_ge(gathered[par][g], (t - par + 2) * (16 * len(GROUPS[g])))
                    if g == 0 and inter:
                        z_banks_free(3)
                    if g >= 2:
                        pe.wait_ge(turned_kept, 4 * t + g - 1)
                    for n, c in enumerate(GROUPS[g]):
                        mm = pe.transpose(bank_t[g % 2][:, n * P:(n + 1) * P], rows[par][:, c, :], ident[:])
                    mm.then_inc(turned, 1)

                def gram_product(t, g):
                    pe.wait_ge(turned_kept, 4 * t + g + 1)
                    if g == 0 and not (isinstance(t, int) and t == 0):
                        pe.wait_ge(y_kept, 8 * t)
                    if g >= 2:
                        pe.wait_ge(quad_done, 4 * t + g - 1)
                    for n, c in enumerate(GROUPS[g]):
                        mm = pe.matmul(bank_g[g % 2][:, n * P:(n + 1) * P], rows_t[:, c, :], gram[:],
                                       start=True, stop=True)
                    mm.then_inc(gram_done, 1)

                def z_banks_free(batches):
                    pe.wait_ge(z_kept_act, 3 * (t - 1) + batches)
                    if any(ZDVE[:batches]):
                        pe.wait_ge(z_kept_dve, ZDVE_TILE * (t - 1) + sum(n > 0 for n in ZDVE[:batches]))

                def interact(batch):
                    if batch == 0:
                        pe.wait_ge(x_placed, t)
                        if not top:
                            pe.wait_ge(sum_x_kept, 4)
                        if load:
                            pe.wait_ge(turned_kept, 4 * (t + 1))
                        if top:
                            pe.wait_ge(z_kept, t - 1)
                            if not (isinstance(t, int) and t == 2):
                                pe.wait_ge(out_kept, t - 2)
                    else:
                        z_banks_free(batch)
                    pe.wait_ge(r_ready, 4 * (t - 1) + -(-sum(ZBATCH[:batch + 1]) * ZBANKS * QUAD // (2 * SPB)))
                    per_bank = ZBATCH[batch]
                    first = sum(ZBATCH[:batch]) * ZBANKS
                    for n in range(per_bank * ZBANKS):
                        mm = pe.matmul(bank_z[:, n // per_bank, (n % per_bank) * ZCOLS:(n % per_bank + 1) * ZCOLS],
                                       r_vec[:, first + n, OTHERS:ZCOLS], r_vec[:, first + n, :], start=True, stop=True)
                    mm.then_inc(z_done, 1)

                def linear(steps):
                    if steps[0] == 0:
                        z_banks_free(3)
                        pe.wait_ge(sumx_placed, t)
                        if not top:
                            pe.wait_ge(wl_centred, 1)
                    for s in steps:
                        mm = pe.matmul(bank_l, zd[:, s, :], wl[:, s, :], start=(s == 0), stop=(s == STEPS - 1))
                    if steps[-1] == STEPS - 1:
                        mm.then_inc(l_done, 1)

                def turn_z():
                    pe.wait_ge(z_scaled, t)
                    for c in range(3):
                        mm = pe.transpose(bank_l[:, c * P:(c + 1) * P], z_row[:, c * P:(c + 1) * P], ident[:])
                    mm.then_inc(z_turned, 1)

                def mix(j):
                    pe.wait_ge(rows_scaled, 4 * t + j + 1)
                    if j < 2 and inter:
                        pe.wait_ge(mix_lo, 8 * t)
                    if j == 1 and top:
                        pe.wait_ge(h1_kept, t - 1)
                    if j >= 2:
                        pe.wait_ge(mix_lo, 8 * t + 2 * (j - 1))
                    wins = [w for w in WINDOWS if w[3] == j]
                    for n, (c, s0, k, _, w0) in enumerate(wins):
                        o = (s0 - j * SPB) * PROJ
                        mm = pe.matmul(bank_m[j % 2][:, o:o + k * PROJ], scaled[:, c, :], wsi_b[:, w0:w0 + k, :],
                                       start=(n == 0), stop=(n == len(wins) - 1), skip_group_check=True)
                    mm.then_inc(mix_done, 1)

                def project(j):
                    for blk in range(2):
                        pe.wait_ge(mix_lo, 8 * t + 2 * j + blk + 1)
                        if j == 0:
                            pe.wait_ge(quad_done, 4 * (t + 1))
                        else:
                            pe.wait_ge(y_kept, 8 * t + 2 * (j - 1) + blk + 1)
                        pe.matmul(bank_g[blk][:], proj_hi[:], mixed[:, j % 2, blk, :], start=True, stop=False)
                        pe.matmul(bank_g[blk][:], proj_lo[:], mixed[:, j % 2, blk, :], start=False, stop=True)\
                            .then_inc(y_done, 1)

                def first_layer(k):
                    if k == 0:
                        if isinstance(t, int) and t == 2:
                            pe.wait_ge(prep, prep_at["w1"])
                        pe.wait_ge(z_kept, t - 1)
                        if load:
                            pe.wait_ge(mix_lo, 8 * t)
                        else:
                            pe.wait_ge(h1_kept, t - 2)
                    dense = [dense_t[:, i, bass.ds((t - 2) * TILE, TILE)] for i in range(2)]
                    for c in range(5):
                        mm = pe.matmul(bank_d[:, k * TILE:(k + 1) * TILE], w1[:, c, k * P:(k + 1) * P],
                                       z_t[:, c, :] if c < 3 else dense[c - 3], start=(c == 0), stop=(c == 4))
                    if k == 3:
                        mm.then_inc(h1_done, 1)

                def second_layer():
                    pe.wait_ge(h1_kept, t - 1)
                    if inter:
                        z_banks_free(3)
                    for k in range(2):
                        for c in range(4):
                            mm = pe.matmul(bank_w[:, k * TILE:(k + 1) * TILE], w2[:, c, k * P:(k + 1) * P], h1[:, c, :],
                                           start=(c == 0), stop=(c == 3))
                    mm.then_inc(h2_done, 1)

                def third_layer():
                    pe.wait_ge(h2_kept, t - 1)
                    for c in range(2):
                        mm = pe.matmul(bank_w[0:1, 0:TILE], w3[:, c:c + 1], h2[:, c, :], start=(c == 0), stop=(c == 1))
                    mm.then_inc(out_done, 1)

                if load:
                    if not inter:
                        for g in range(len(GROUPS)):
                            turn(t, par, g)
                        gram_product(t, 0)
                        gram_product(t, 1)
                    gram_product(t, 2)
                    gram_product(t, 3)
                if top:
                    first_layer(0)
                if inter:
                    interact(0)
                if top:
                    first_layer(1)
                if load and not inter:
                    fold(range(0, 1))
                    fold(range(1, 6))
                if load:
                    mix(0)
                if top:
                    first_layer(2)
                if load and not inter:
                    add_up_x(0)
                if top:
                    first_layer(3)
                if load:
                    project(0)
                if inter:
                    interact(1)
                if load:
                    mix(1)
                if load and not inter:
                    fold(range(6, STEPS))
                if load:
                    mix(2)
                if inter:
                    interact(2)
                if load:
                    project(1)
                    mix(3)
                if more:
                    turn(t + 1, 1 - par, 0)
                if inter:
                    linear(range(0, 1))
                if load and not inter:
                    add_up_x(1)
                if load:
                    project(2)
                if more:
                    turn(t + 1, 1 - par, 1)
                if inter:
                    linear(range(1, 3))
                if load and not inter:
                    add_up_x(2)
                if inter:
                    linear(range(3, 4))
                if load:
                    project(3)
                if inter:
                    linear(range(4, 5))
                if more:
                    turn(t + 1, 1 - par, 2)
                if inter:
                    linear(range(5, 7))
                if load and not inter:
                    add_up_x(3)
                if inter:
                    linear(range(7, STEPS))
                if more:
                    turn(t + 1, 1 - par, 3)
                if inter and not top:
                    fold_bl()
                if top:
                    second_layer()
                if more:
                    gram_product(t + 1, 0)
                    gram_product(t + 1, 1)
                if inter:
                    turn_z()
                if top:
                    third_layer()

            over_tiles(pe, tile_work)

        @block.scalar
        def _(act):
            act.wait_ge(prep, prep_at["constants"])
            for j in range(4):
                act.wait_ge(pe_prep, 4 + j)
                for n in range(4):
                    t = 4 * j + n
                    ins = nc.scalar.activation(y_sq[:, j // 2, j % 2, n * E:(n + 1) * E], bank_z[:, j, n * E:(n + 1) * E],
                                               ACT.Square, accum_out=x_var[:, t:t + 1])
                ins.then_inc(x_squared, 1)
                act.wait_ge(x_squared, j + 1)
                nc.scalar.activation(x_std[:, 4 * j:4 * j + 4], x_var[:, 4 * j:4 * j + 4], ACT.Sqrt, bias=eps[:],
                                     scale=1.0 / E).then_inc(act_prep, 1)
            act.wait_ge(prep, prep_at["end"])

            def keep_sum_x(j):
                act.wait_ge(sum_x_done, j + 1)
                nc.scalar.copy(sum_x[PROJ:PROJ + 1, j * BANK:(j + 1) * BANK], bank_w[PROJ:PROJ + 1, :])\
                    .then_inc(sum_x_kept, 1)

            def scale_linear(steps):
                if steps[0] == 0:
                    act.wait_ge(fold_done, 1)
                for t in steps:
                    nc.scalar.activation(wl[:, t, :], wl[:, t, :], ACT.Copy, scale=col["gsi_q"][:, t:t + 1],
                                         accum_out=means[:, t:t + 1]).then_inc(wl_scaled, 1)

            def centre_linear():
                act.wait_ge(prep, prep_at["wl_means"])
                act.wait_ge(wl_scaled, QPK)
                for t in range(STEPS):
                    ins = nc.scalar.activation(wl[:, t, :], wl[:, t, :], ACT.Identity, bias=means[:, t:t + 1])
                ins.then_inc(wl_centred, 1)

            def tile_work(t, par, more, load, inter, top):
                def keep_z(batch):
                    act.wait_ge(z_done, 3 * (t - 1) + batch + 1)
                    if batch == 0 and top:
                        act.wait_ge(l_done, t - 1)
                    for to, src in z_moves(batch)[0]:
                        ins = nc.scalar.copy(to, src)
                    ins.then_inc(z_kept_act, 1)

                def square(j):
                    for blk in range(2):
                        act.wait_ge(y_kept, 8 * t + 2 * j + blk + 1)
                        if blk == 0 and (inter or j >= 2):
                            act.wait_ge(y_var_done, 4 * t + j - 1)
                        nc.scalar.activation(y_sq[:, j % 2, blk, :], y[:, Y_PART[j], blk, :], ACT.Square)\
                            .then_inc(y_squared, 1)

                def y_root(t, j, inter):
                    act.wait_ge(y_var_done, 4 * t + j + 1)
                    if inter:
                        act.wait_ge(y_r_done, 4 * (t - 1) + j + 1)
                    nc.scalar.activation(y_std[:, j, :], y_var[:, j, :], ACT.Sqrt, bias=eps[:], scale=1.0 / PROJ)\
                        .then_inc(y_std_done, 1)

                def keep_high(j):
                    act.wait_ge(mix_done, 4 * t + j + 1)
                    for blk in range(2):
                        if inter or j >= 2:
                            act.wait_ge(y_done, 8 * t + 2 * j + blk - 3)
                        own = slice(D * blk, D * (blk + 1))
                        nc.scalar.copy(mixed[own, j % 2, blk, :], bank_m[j % 2][own, :]).then_inc(mix_hi, 1)

                def relu_1():
                    act.wait_ge(h1_done, t - 1)
                    if not (isinstance(t, int) and t == 2):
                        act.wait_ge(h2_done, t - 2)
                    for k in range(4):
                        ins = nc.scalar.activation(h1[:, k, :], bank_d[:, k * TILE:(k + 1) * TILE], ACT.Relu,
                                                   bias=b1[:, k:k + 1])
                    ins.then_inc(h1_kept, 1)

                def relu_2():
                    act.wait_ge(h2_done, t - 1)
                    if not (isinstance(t, int) and t == 2):
                        act.wait_ge(out_done, t - 2)
                    for k in range(2):
                        ins = nc.scalar.activation(h2[:, k, :], bank_w[:, k * TILE:(k + 1) * TILE], ACT.Relu,
                                                   bias=col["b2"][:, k:k + 1])
                    ins.then_inc(h2_kept, 1)

                def keep_out():
                    act.wait_ge(out_done, t - 1)
                    nc.scalar.copy(out_row[:, bass.ds((t - 2) * TILE, TILE)], bank_w[0:1, 0:TILE]).then_inc(out_kept, 1)

                def keep_turned(t, g):
                    act.wait_ge(turned, 4 * t + g + 1)
                    if not (isinstance(t, int) and t == 0):
                        act.wait_ge(gram_done, 4 * (t - 1) + g + 1)
                    cs = GROUPS[g]
                    nc.scalar.copy(rows_t[:, cs[0]:cs[-1] + 1, :],
                                   bank_t[g % 2][:, 0:len(cs) * P].rearrange("p (c n) -> p c n", n=P))\
                        .then_inc(turned_kept, 1)

                def row_root():
                    act.wait_ge(var_done, t + 1)
                    if inter:
                        act.wait_ge(rstd_done, t)
                    nc.scalar.activation(row_std[:], row_var[:], ACT.Sqrt, bias=eps[:]).then_inc(row_std_done, 1)

                def place_sum_x():
                    if top:
                        act.wait_ge(l_done, t - 1)
                    nc.scalar.copy(zd[PROJ:PROJ + 1, STEPS - 1, :],
                                   sum_x[PROJ:PROJ + 1, bass.ds((t - 1) * TILE, TILE)]).then_inc(sumx_placed, 1)

                def place_x():
                    if inter:
                        act.wait_ge(z_done, 3 * t)
                    nc.scalar.copy(r_vec[:, :, 0:QUAD], x_t[:, bass.ds(t * TILE, TILE)].rearrange("p (g j) -> p g j", j=QUAD))\
                        .then_inc(x_placed, 1)

                def linear_root():
                    act.wait_ge(l_done, t)
                    nc.scalar.activation(l_sq[:], bank_l, ACT.Square, accum_out=l_var[:]).then_inc(l_var_done, 1)
                    act.wait_ge(l_var_done, t)
                    if top:
                        act.wait_ge(l_r_done, t - 1)
                    nc.scalar.activation(l_std[:], l_var[:], ACT.Sqrt, bias=eps[:], scale=1.0 / MAXD)\
                        .then_inc(l_std_done, 1)

                def scale_z():
                    act.wait_ge(l_r_done, t)
                    if top:
                        act.wait_ge(z_turned, t - 1)
                    nc.scalar.activation(z_row[:], bank_l[:, 0:USED], ACT.Copy, scale=l_r[:]).then_inc(z_scaled, 1)

                def keep_turned_z():
                    act.wait_ge(z_turned, t)
                    if top:
                        act.wait_ge(h1_done, t - 1)
                    nc.scalar.copy(z_t[:], bank_l[:, 0:USED].rearrange("p (c b) -> p c b", c=3)).then_inc(z_kept, 1)

                if load:
                    if not inter:
                        for g in range(len(GROUPS)):
                            keep_turned(t, g)
                if inter and not top:
                    centre_linear()
                if inter:
                    y_root(t - 1, 3, top)
                if load:
                    row_root()
                if inter:
                    place_sum_x()
                    keep_z(0)
                if load:
                    keep_high(0)
                if load and not inter:
                    keep_sum_x(0)
                if top:
                    relu_1()
                if load:
                    square(0)
                if inter:
                    keep_z(1)
                if load:
                    keep_high(1)
                    keep_high(2)
                if inter:
                    keep_z(2)
                if load and not inter:
                    scale_linear(range(0, 4))
                if load:
                    keep_high(3)
                if more:
                    keep_turned(t + 1, 0)
                if load:
                    y_root(t, 0, inter)
                    square(1)
                if more:
                    keep_turned(t + 1, 1)
                if load and not inter:
                    keep_sum_x(1)
                if load:
                    square(2)
                if load and not inter:
                    scale_linear(range(4, QPK))
                if load:
                    place_x()
                    y_root(t, 1, inter)
                if load and not inter:
                    keep_sum_x(2)
                if load:
                    square(3)
                    y_root(t, 2, inter)
                if inter:
                    linear_root()
                    scale_z()
                if more:
                    keep_turned(t + 1, 2)
                if top:
                    relu_2()
                if load and not inter:
                    keep_sum_x(3)
                if inter:
                    keep_turned_z()
                if more:
                    keep_turned(t + 1, 3)
                if top:
                    keep_out()

            over_tiles(act, tile_work)


def column(a, n=1):
    return np.asarray(a).reshape(n, P).T


def laid_out(x):
    f32 = np.float32
    tables = [np.asarray(x[f"tbl_{f}"]) for f in range(N_SP)]
    first_row = np.cumsum([0] + [t.shape[0] for t in tables])[:-1]
    feature = (np.arange(CHUNKS * P) % N_SP).reshape(CHUNKS, P)
    ids = np.asarray(x["ids"]).reshape(TILES, MIX_BANKS, 2, SPB, N_SP).transpose(0, 2, 1, 3, 4)
    ids = ids.reshape(TILES, 2, CHUNKS, P).transpose(3, 0, 2, 1)
    wsi = np.asarray(x["L0_rec_Wsi"])
    wsi_b = np.zeros((P, WIN_COLS, PROJ), f32)
    for c, s0, k, bank, w0 in WINDOWS:
        for r in range(P):
            s, n = divmod(c * P + r, N_SP)
            if s0 <= s < s0 + k and s // SPB == bank:
                wsi_b[r, w0 + s - s0] = wsi[:, n]
    lin = np.asarray(x["L0_rec_Wl"])
    gsi, bsi = np.asarray(x["L0_rec_gsi"]), np.asarray(x["L0_rec_bsi"])
    wl = np.zeros((P, STEPS, MAXD), f32)
    gsi_q = np.ones((P, STEPS), f32)
    bsi_q = np.zeros((P, STEPS), f32)
    mask_a = np.zeros((P, 64), f32)
    mask_b = np.zeros((P, STEPS, 64), f32)
    for k in range(4):
        quarter = slice(PROJ * k, PROJ * (k + 1))
        mask_a[quarter, 0:PROJ] = np.eye(PROJ, dtype=f32)
        for t in range(QPK):
            q = QPK * k + t
            gsi_q[quarter, t] = gsi[q]
            bsi_q[quarter, t] = bsi[q]
            mask_b[quarter, t, q] = 1.0
            for p in range(q + 1, PROJ):
                wl[PROJ * k + p, t] = lin[:, (p + 1) * p // 2 + q + 1]
    for p in range(PROJ):
        wl[p, QPK] = lin[:, (p + 1) * p // 2]
    mask_b[0:PROJ, QPK, PROJ] = 1.0
    cols = {
        "gd": column(x["L0_rec_gd"]), "bd": column(x["L0_rec_bd"]),
        "gsi_p": np.tile(gsi, 4)[:, None], "bsi_p": np.tile(bsi, 4)[:, None],
        "gsi_q": gsi_q, "bsi_q": bsi_q,
        "gl": column(np.asarray(x["L0_rec_gl"])[:USED], 3), "bl": column(np.asarray(x["L0_rec_bl"])[:USED], 3),
        "b1": column(x["b_top1"], 4), "b2": column(x["b_top2"], 2),
    }
    top1 = np.asarray(x["W_top1"])
    top1 = np.concatenate([top1[:USED], top1[MAXD:]])
    dense_t = np.asarray(x["r_dense_t"]).T
    ws = np.asarray(x["L0_rec_Ws"])
    arrays = {
        "table": np.concatenate(tables),
        "ids": ids.reshape(P, -1),
        "row_base": np.repeat(first_row[feature].T, 2, axis=1).astype(np.int32),
        "ident": np.eye(P, dtype=f32),
        "ws_t": np.concatenate([ws.T, ws.T]),
        "gs_row": np.broadcast_to(np.asarray(x["L0_rec_gs"]), (P, E)),
        "bs_row": np.broadcast_to(np.asarray(x["L0_rec_bs"]), (N_SP, E)),
        "wsi_n": wsi.T, "wsi_b": wsi_b, "wl": wl, "mask_a": mask_a, "mask_b": mask_b,
        "wd_t": np.asarray(x["L0_rec_Wd"]).T.reshape(2, P, E).transpose(1, 0, 2),
        "dense_t": dense_t.reshape(2, P, B).transpose(1, 0, 2),
        "cols": np.concatenate([cols[name] for name, _ in COLS], axis=1),
        "w1": top1.reshape(5, P, H1).transpose(1, 0, 2),
        "w2": np.asarray(x["W_top2"]).reshape(4, P, H2).transpose(1, 0, 2),
        "w3": column(x["W_top3"], 2),
    }
    return {name: np.ascontiguousarray(a) for name, a in arrays.items()}


def kernel(**inputs):
    import concourse.bacc as bacc
    from concourse.bass_utils import run_bass_kernel_spmd

    nc = bacc.Bacc("TRN2", target_bir_lowering=False, num_devices=1)
    arrays = laid_out(inputs)
    io = {name: nc.dram_tensor(f"in_{name}", a.shape, mybir.dt.from_np(a.dtype), kind="ExternalInput").ap()
          for name, a in arrays.items()}
    io["out"] = nc.dram_tensor("out", (B, 1), F32, kind="ExternalOutput").ap()
    tower(nc, io)
    r = run_bass_kernel_spmd(nc, [{f"in_{name}": a for name, a in arrays.items()}], core_ids=[0])
    return r.results[0]["out"]
```
